# Optimizing a Trainium2 kernel written in Bass

```python
import numpy as np
import jax
import jax.numpy as jnp

def _softmax(x, axis=-1):
    return jax.nn.softmax(x, axis=axis)

def _gelu(x):
    return jax.nn.gelu(x, approximate=True)

def _silu(x):
    return jax.nn.silu(x)

def _sigmoid(x):
    return jax.nn.sigmoid(x)

def _layernorm(x, axis=-1, eps=1e-05):
    m = jnp.mean(x, axis=axis, keepdims=True)
    v = jnp.var(x, axis=axis, keepdims=True)
    return (x - m) / jnp.sqrt(v + eps)

def _scatter_add(tgt, idx, src, axis=0):
    return tgt.at[idx].add(src)

def _segment_sum(src, seg, n):
    return jax.ops.segment_sum(src, seg, n)
kernel_name = 'mk_gnn_resnorm_d4_gnn_r8_b7263a'

def setup_inputs(seed: int=0):
    np.random.seed(seed)
    _w = jnp.asarray

    def _rec_inputs():
        import jax
        import jax.numpy as jnp
        _gk = jax.random.key(seed)
        x = -0.000202 + 1 * jax.random.normal(jax.random.fold_in(_gk, 1), (6250, 128), jnp.float32)
        src = jax.random.randint(jax.random.fold_in(_gk, 2), (200000,), 0, 6250, jnp.int32)
        dst = jnp.minimum((6250 * jax.random.uniform(jax.random.fold_in(_gk, 3), (200000,)) ** 2.0).astype(jnp.int32), 49999)
        _o = jnp.argsort(dst, stable=True)
        src = src[_o]
        dst = dst[_o]
        edge_attr_64 = jax.random.uniform(jax.random.fold_in(_gk, 12), (200000, 64), jnp.float32, 0.0, 1)
        edge_type_40 = jax.random.randint(jax.random.fold_in(_gk, 14), (200000,), 0, 40, jnp.int32)
        edge_weight = jax.random.uniform(jax.random.fold_in(_gk, 15), (200000,), jnp.float32, 0.0, 0.999998)
        return (x, src, dst, edge_attr_64, edge_type_40, edge_weight)
    x, src, dst, edge_attr_64, edge_type_40, edge_weight = _rec_inputs()

    def _L0_gnn_setup():
        import jax, jax.numpy as jnp
        import numpy as np
        N_NODES = 6250
        N_EDGES = 200000
        IN_FEAT = 128
        OUT_FEAT = 128
        NUM_RELS = 40
        key = jax.random.key(seed)
        ks = jax.random.split(key, 8)
        h = jax.random.normal(ks[0], (N_NODES, IN_FEAT), dtype=jnp.float32)
        W = jax.random.normal(ks[1], (OUT_FEAT, IN_FEAT), dtype=jnp.float32) / np.sqrt(IN_FEAT)
        attn_w = jax.random.normal(ks[2], (1, 2 * OUT_FEAT), dtype=jnp.float32) / np.sqrt(2 * OUT_FEAT)
        rel_emb = jax.random.normal(ks[3], (NUM_RELS, 1), dtype=jnp.float32)
        rel_emb = rel_emb.at[0].set(0.0)
        stdv = 1.0 / np.sqrt(OUT_FEAT)
        bias_w = jax.random.uniform(ks[4], (OUT_FEAT,), minval=-stdv, maxval=stdv, dtype=jnp.float32)
        src = jax.random.randint(ks[5], (N_EDGES,), 0, N_NODES, dtype=jnp.int32)
        dst = jax.random.randint(ks[6], (N_EDGES,), 0, N_NODES, dtype=jnp.int32)
        etype = jax.random.randint(ks[7], (N_EDGES,), 0, NUM_RELS, dtype=jnp.int32)
        return {'h': h, 'W': W, 'attn_w': attn_w, 'rel_emb': rel_emb, 'bias_w': bias_w, 'src': src, 'dst': dst, 'etype': etype}
    _L0_gnn_all = _L0_gnn_setup()
    _L0_gnn_in = {k: v for k, v in _L0_gnn_all.items() if k in ('W', 'attn_w', 'rel_emb', 'bias_w')}
    del _L0_gnn_all

    def _L1_gnn_setup():
        import jax, jax.numpy as jnp
        import numpy as np
        N_NODES = 6250
        N_EDGES = 100000
        DIM_IN = 128
        DIM_OUT = 128
        key = jax.random.key(seed)
        k1, k2, k3, k4 = jax.random.split(key, 4)
        node_feature = jax.random.normal(k1, (N_NODES, DIM_IN), dtype=jnp.float32)
        edge_index = jax.random.randint(k2, (2, N_EDGES), 0, N_NODES, dtype=jnp.int64)
        W_l = jax.random.normal(k3, (DIM_OUT, DIM_IN), dtype=jnp.float32) * (1.0 / np.sqrt(DIM_IN))
        W_r = jax.random.normal(k4, (DIM_OUT, DIM_IN), dtype=jnp.float32) * (1.0 / np.sqrt(DIM_IN))
        return {'node_feature': node_feature, 'edge_index': edge_index, 'W_l': W_l, 'W_r': W_r}
    _L1_gnn_all = _L1_gnn_setup()
    _L1_gnn_in = {k: v for k, v in _L1_gnn_all.items() if k in ('W_l', 'W_r')}
    del _L1_gnn_all

    def _L2_gnn_setup():
        import jax, jax.numpy as jnp
        import numpy as np
        N_NODES = 12500
        N_EDGES = 80000
        D_IN = 128
        HIDDEN = 128
        OUT = 128

        def _graph_conv(x, src, dst, w, W_rel, b_rel, W_root, n_nodes):
            msg = x[src] * w[:, None]
            agg = jax.ops.segment_sum(msg, dst, num_segments=n_nodes)
            return agg @ W_rel.T + b_rel + x @ W_root.T
        key = jax.random.key(seed)
        ks = jax.random.split(key, 16)
        x = jax.random.normal(ks[0], (N_NODES, D_IN), dtype=jnp.float32)
        edge_index = jax.random.randint(ks[1], (2, N_EDGES), 0, N_NODES, dtype=jnp.int64)
        edge_weight = jax.random.uniform(ks[2], (N_EDGES,), dtype=jnp.float32)

        def lin(k, fan_in, fan_out):
            s = 1.0 / np.sqrt(fan_in)
            return jax.random.uniform(k, (fan_out, fan_in), minval=-s, maxval=s, dtype=jnp.float32)
        params = {'W_rel1': lin(ks[3], D_IN, HIDDEN), 'b_rel1': jnp.zeros((HIDDEN,), jnp.float32), 'W_root1': lin(ks[4], D_IN, HIDDEN), 'W_rel2': lin(ks[5], HIDDEN, HIDDEN), 'b_rel2': jnp.zeros((HIDDEN,), jnp.float32), 'W_root2': lin(ks[6], HIDDEN, HIDDEN), 'W_rel3': lin(ks[7], HIDDEN, OUT), 'b_rel3': jnp.zeros((OUT,), jnp.float32), 'W_root3': lin(ks[8], HIDDEN, OUT)}
        return {'x': x, 'edge_index': edge_index, 'edge_weight': edge_weight, **params}
    _L2_gnn_all = _L2_gnn_setup()
    _L2_gnn_in = {k: v for k, v in _L2_gnn_all.items() if k in ('W_rel1', 'b_rel1', 'W_root1', 'W_rel2', 'b_rel2', 'W_root2', 'W_rel3', 'b_rel3', 'W_root3')}
    del _L2_gnn_all

    def _L3_gnn_setup():
        import jax, jax.numpy as jnp
        import numpy as np
        N_NODES = 5000
        N_EDGES = 80000
        IN_CH = 128
        OUT_CH = 128
        NUM_RBF = 64
        key = jax.random.key(seed)
        ks = jax.random.split(key, 8)
        x = jax.random.normal(ks[0], (N_NODES, IN_CH), dtype=jnp.float32)
        edge_index = jax.random.randint(ks[1], (2, N_EDGES), 0, N_NODES, dtype=jnp.int64)
        edge_rbf = jax.random.uniform(ks[2], (N_EDGES, NUM_RBF), dtype=jnp.float32)
        s1 = 1.0 / np.sqrt(NUM_RBF)
        s2 = 1.0 / np.sqrt(OUT_CH)
        sl = 1.0 / np.sqrt(IN_CH)
        W1 = jax.random.normal(ks[3], (NUM_RBF, OUT_CH), dtype=jnp.float32) * s1
        b1 = jnp.zeros((OUT_CH,), dtype=jnp.float32)
        W2 = jax.random.normal(ks[4], (OUT_CH, OUT_CH), dtype=jnp.float32) * s2
        b2 = jnp.zeros((OUT_CH,), dtype=jnp.float32)
        Wl = jax.random.normal(ks[5], (IN_CH, OUT_CH), dtype=jnp.float32) * sl
        bl = jnp.zeros((OUT_CH,), dtype=jnp.float32)
        return {'x': x, 'edge_index': edge_index, 'edge_rbf': edge_rbf, 'W1': W1, 'b1': b1, 'W2': W2, 'b2': b2, 'Wl': Wl, 'bl': bl}
    _L3_gnn_all = _L3_gnn_setup()
    _L3_gnn_in = {k: v for k, v in _L3_gnn_all.items() if k in ('W1', 'b1', 'W2', 'b2', 'Wl', 'bl')}
    del _L3_gnn_all
    return {'x': x, 'src': src, 'dst': dst, 'edge_attr_64': edge_attr_64, 'edge_type_40': edge_type_40, 'edge_weight': edge_weight, 'L0_gnn_W': _L0_gnn_in['W'], 'L0_gnn_attn_w': _L0_gnn_in['attn_w'], 'L0_gnn_rel_emb': _L0_gnn_in['rel_emb'], 'L0_gnn_bias_w': _L0_gnn_in['bias_w'], 'L1_gnn_W_l': _L1_gnn_in['W_l'], 'L1_gnn_W_r': _L1_gnn_in['W_r'], 'L2_gnn_W_rel1': _L2_gnn_in['W_rel1'], 'L2_gnn_b_rel1': _L2_gnn_in['b_rel1'], 'L2_gnn_W_root1': _L2_gnn_in['W_root1'], 'L2_gnn_W_rel2': _L2_gnn_in['W_rel2'], 'L2_gnn_b_rel2': _L2_gnn_in['b_rel2'], 'L2_gnn_W_root2': _L2_gnn_in['W_root2'], 'L2_gnn_W_rel3': _L2_gnn_in['W_rel3'], 'L2_gnn_b_rel3': _L2_gnn_in['b_rel3'], 'L2_gnn_W_root3': _L2_gnn_in['W_root3'], 'L3_gnn_W1': _L3_gnn_in['W1'], 'L3_gnn_b1': _L3_gnn_in['b1'], 'L3_gnn_W2': _L3_gnn_in['W2'], 'L3_gnn_b2': _L3_gnn_in['b2'], 'L3_gnn_Wl': _L3_gnn_in['Wl'], 'L3_gnn_bl': _L3_gnn_in['bl']}

def reference(x, src, dst, edge_attr_64, edge_type_40, edge_weight, L0_gnn_W, L0_gnn_attn_w, L0_gnn_rel_emb, L0_gnn_bias_w, L1_gnn_W_l, L1_gnn_W_r, L2_gnn_W_rel1, L2_gnn_b_rel1, L2_gnn_W_root1, L2_gnn_W_rel2, L2_gnn_b_rel2, L2_gnn_W_root2, L2_gnn_W_rel3, L2_gnn_b_rel3, L2_gnn_W_root3, L3_gnn_W1, L3_gnn_b1, L3_gnn_W2, L3_gnn_b2, L3_gnn_Wl, L3_gnn_bl):
    import jax
    import jax.numpy as jnp

    def _L0_gnn_ref(h, W, attn_w, rel_emb, bias_w, src, dst, etype):
        import jax, jax.numpy as jnp
        import numpy as np
        N_NODES = 6250
        N_EDGES = 200000
        IN_FEAT = 128
        OUT_FEAT = 128
        NUM_RELS = 40
        n = h.shape[0]
        out_feat = W.shape[0]
        z = h @ W.T
        w1 = attn_w[0, :out_feat]
        w2 = attn_w[0, out_feat:]
        s_src = z @ w1
        s_dst = z @ w2
        e = jax.nn.leaky_relu(s_src[src] + s_dst[dst], negative_slope=0.01)
        rel_alpha = rel_emb[etype, 0]
        m = jax.ops.segment_max(e, dst, num_segments=n)
        num = jnp.exp(e - m[dst])
        den = jax.ops.segment_sum(num, dst, num_segments=n)
        alpha = num / den[dst]
        w_e = (rel_alpha * alpha)[:, None]
        h_agg = jax.ops.segment_sum(w_e * z[src], dst, num_segments=n)
        return h_agg + bias_w

    def _L1_gnn_ref(node_feature, edge_index, W_l, W_r):
        import jax, jax.numpy as jnp
        import numpy as np
        N_NODES = 6250
        N_EDGES = 100000
        DIM_IN = 128
        DIM_OUT = 128
        n = node_feature.shape[0]
        src = edge_index[0]
        dst = edge_index[1]
        msgs = node_feature[src]
        summed = jax.ops.segment_sum(msgs, dst, num_segments=n)
        deg = jax.ops.segment_sum(jnp.ones((msgs.shape[0],), dtype=node_feature.dtype), dst, num_segments=n)
        aggr = summed / jnp.maximum(deg, 1.0)[:, None]
        return aggr @ W_l.T + node_feature @ W_r.T

    def _L2_gnn_ref(x, edge_index, edge_weight, W_rel1, b_rel1, W_root1, W_rel2, b_rel2, W_root2, W_rel3, b_rel3, W_root3):
        import jax, jax.numpy as jnp
        import numpy as np
        N_NODES = 12500
        N_EDGES = 80000
        D_IN = 128
        HIDDEN = 128
        OUT = 128

        def _graph_conv(x, src, dst, w, W_rel, b_rel, W_root, n_nodes):
            msg = x[src] * w[:, None]
            agg = jax.ops.segment_sum(msg, dst, num_segments=n_nodes)
            return agg @ W_rel.T + b_rel + x @ W_root.T
        src, dst = (edge_index[0], edge_index[1])
        n = x.shape[0]
        h = jax.nn.relu(_graph_conv(x, src, dst, edge_weight, W_rel1, b_rel1, W_root1, n))
        h = jax.nn.relu(_graph_conv(h, src, dst, edge_weight, W_rel2, b_rel2, W_root2, n))
        h = _graph_conv(h, src, dst, edge_weight, W_rel3, b_rel3, W_root3, n)
        return h

    def _L3_gnn_ref(x, edge_index, edge_rbf, W1, b1, W2, b2, Wl, bl):
        import jax, jax.numpy as jnp
        import numpy as np
        N_NODES = 5000
        N_EDGES = 80000
        IN_CH = 128
        OUT_CH = 128
        NUM_RBF = 64
        weight = jnp.maximum(edge_rbf @ W1 + b1, 0.0) @ W2 + b2
        h = x @ Wl + bl
        row, col = (edge_index[0], edge_index[1])
        msg = h[col] * weight
        out = jax.ops.segment_sum(msg, row, num_segments=x.shape[0])
        return out
    edge_index = jnp.stack([src, dst])
    x = _layernorm(x + _L0_gnn_ref(x, L0_gnn_W, L0_gnn_attn_w, L0_gnn_rel_emb, L0_gnn_bias_w, src, dst, edge_type_40), axis=-1)
    x = _layernorm(x + _L1_gnn_ref(x, edge_index, L1_gnn_W_l, L1_gnn_W_r), axis=-1)
    x = _layernorm(x + _L2_gnn_ref(x, edge_index, edge_weight, L2_gnn_W_rel1, L2_gnn_b_rel1, L2_gnn_W_root1, L2_gnn_W_rel2, L2_gnn_b_rel2, L2_gnn_W_root2, L2_gnn_W_rel3, L2_gnn_b_rel3, L2_gnn_W_root3), axis=-1)
    x = _layernorm(x + _L3_gnn_ref(x, edge_index, edge_attr_64, L3_gnn_W1, L3_gnn_b1, L3_gnn_W2, L3_gnn_b2, L3_gnn_Wl, L3_gnn_bl), axis=-1)
    return x

_drawn_inputs = setup_inputs


def setup_inputs(seed=0):
    import zlib

    import numpy as np

    out = dict(_drawn_inputs(seed))
    spreads = {'L2_gnn_b_rel1': (0.0, 0.1),
     'L2_gnn_b_rel2': (0.0, 0.1),
     'L2_gnn_b_rel3': (0.0, 0.1),
     'L3_gnn_b1': (0.0, 0.1),
     'L3_gnn_b2': (0.0, 0.1),
     'L3_gnn_bl': (0.0, 0.1)}
    factors = {}
    for name, (base, spread) in spreads.items():
        noise = np.random.default_rng([zlib.crc32(name.encode()), seed]).standard_normal(out[name].shape)
        drawn = base * np.exp(spread * noise) if base else spread * noise
        out[name] = jnp.asarray(drawn.astype(out[name].dtype))
    for name, factor in factors.items():
        out[name] = (out[name] * factor).astype(out[name].dtype)
    return out
```

```python
from contextlib import ExitStack

import concourse.bass as bass
import concourse.mybir as mybir
from concourse.alu_op_type import AluOpType as ALU

P = 128
F = 128
N_NODES = 6250
N_EDGES = 200000
N_RELS = 40
N_RBF = 64
NB = -(-N_NODES // P)
NP_ = NB * P
TILES = 8
GE = TILES * P
NG = -(-N_EDGES // GE)
EP = NG * GE
SLOTS = 4
TURNS = NG // SLOTS
PAD_NODE = NP_ - 1
assert NG % SLOTS == 0 and TURNS == NB and PAD_NODE >= N_NODES
HG = NG // 2
ZW = F + 2
MW = F + 1
HUGE = 3.0e38
TINY = 1.0e-30
EPS = 1.0e-5
SLOPE = 0.01
C_IDENT, C_TRI, C_ONES, C_NODE, C_GROUP = 0, P, 2 * P, 3 * P, 3 * P + NB
C_WIDTH = C_GROUP + 2

f32 = mybir.dt.float32
i32 = mybir.dt.int32
u32 = mybir.dt.uint32
AX = mybir.AxisListType.X
ACT = mybir.ActivationFunctionType


def build_program(nc, T, out):
    ctx = ExitStack()
    with ctx:
        def sb(name, shape, dt=f32):
            return ctx.enter_context(nc.sbuf_tensor(name, shape, dt))

        live = []

        def sem(name):
            live.append(nc.alloc_semaphore(name=name))
            return live[-1]

        def release_semaphores():
            with nc.Block() as block:
                @block.gpsimd
                def _(e):
                    nc.clear_and_free_semaphores(list(live))
                    e.drain()
            live.clear()

        def dram(name, shape, dt=f32):
            return nc.dram_tensor(name, shape, dt, kind="Internal").ap()

        consts = sb("consts", [P, C_WIDTH])
        ident = consts[:, C_IDENT:C_IDENT + P]
        tri = consts[:, C_TRI:C_TRI + P]
        ones = consts[:, C_ONES:C_ONES + P]
        node_id = consts[:, C_NODE:C_NODE + NB]
        group_at = consts[:, C_GROUP:C_GROUP + 2]
        iota = sb("iota", [P, NP_])
        names = ["L0_gnn_W", "L0_gnn_Wt", "L1_gnn_W_lt", "L1_gnn_W_rt", "L2_gnn_W_rel1t", "L2_gnn_W_root1t",
                 "L2_gnn_W_rel2t", "L2_gnn_W_root2t", "L2_gnn_W_rel3t", "L2_gnn_W_root3t",
                 "L3_gnn_W1d", "L3_gnn_W2", "L3_gnn_Wl"]
        W = {n: sb("w_" + n, [P, ZW if n == "L0_gnn_Wt" else F]) for n in names}
        attn = sb("attn", [P, 2])
        bias_names = ["L0_gnn_bias_w", "L2_gnn_b_rel1", "L2_gnn_b_rel2", "L2_gnn_b_rel3", "L3_gnn_b2", "L3_gnn_bl"]
        bias = {n: sb("b_" + n, [P, F]) for n in bias_names}
        b1_col = sb("b1_col", [P, 1])
        rel_row = sb("rel_row", [P, N_RELS])
        src_i = sb("src_i", [P, NG * TILES], i32)
        dst_f = sb("dst_f", [P, NG * TILES])
        type_f = sb("type_f", [P, NG * TILES])
        weight = sb("weight", [P, NG * TILES])
        pos = type_f
        pos_i = sb("pos_i", [P, NG * TILES], i32)
        X = sb("X", [P, NB * F])
        A = sb("A", [P, NB * ZW])
        H = sb("H", [P, NB * F])
        src_block, mask, cum = (H[:, k * NG * TILES:(k + 1) * NG * TILES] for k in range(3))
        rows = sb("rows", [P, SLOTS, TILES, ZW])
        idx = sb("idx", [P, SLOTS, TILES], i32)
        onehot = sb("onehot", [P, TILES, P])
        onehot_t = sb("onehot_t", [P, GE])
        dst_bc = sb("dst_bc", [P, 2, GE], i32)
        table_dst = sb("table_dst", [1, 2 * NG], i32)
        table_src = sb("table_src", [1, 2 * NG], i32)
        small = sb("small", [P, 64])
        tot = sb("tot", [P, NB])
        base = sb("base", [P, NB])
        start_of = sb("start_of", [P, NB])
        end_of = sb("end_of", [P, NB])
        stats = sb("stats", [P, 6])
        mv = sb("mv", [P, NB, 2])
        rstd = sb("rstd", [P, NB])
        tT = sb("tT", [P, 2, 2 * P])
        bank = [ctx.enter_context(nc.psum_tensor(f"bank{k}", [P, 512], f32)) for k in range(8)]

        def A_(w):
            return A[:, 0:NB * w].rearrange("p (b f) -> p b f", f=w)

        Xv = X[:, :].rearrange("p (b f) -> p b f", f=F)
        z_table = dram("z_table", (NP_, ZW))
        x_tables = [dram(f"x_table{k}", (NP_, F)) for k in range(4)]
        sorted_rows = dram("sorted_rows", (EP, MW))
        range_dst = dram("range_dst", (NG, 2), i32)
        range_src = dram("range_src", (NG, 2), i32)

        s_small, s_edge, s_iota, s_w = sem("s_small"), sem("s_edge"), sem("s_iota"), sem("s_w")
        s_gd, s_rng, s_rng_out, s_rng_in = sem("s_gd"), sem("s_rng"), sem("s_rng_out"), sem("s_rng_in")
        n_w = [0]
        gd = onehot[:, :, :].rearrange("p a b -> p (a b)").bitcast(i32)
        with nc.Block() as block:
            @block.sync
            def _(e):
                e.dma_start(consts[:, :], T["consts"]).then_inc(s_small, 16)
                e.dma_start(src_i[:, :], T["src_c"]).then_inc(s_edge, 16)
                e.dma_start(dst_bc[:, 0, 0:GE], T["dst_row"][0:P, :]).then_inc(s_gd, 16)
                e.dma_start(dst_bc[0:NG - P, 1, 0:GE], T["dst_row"][P:NG, :]).then_inc(s_gd, 16)
                e.dma_start(X[:, :].rearrange("p (b f) -> p b f", f=F),
                            T["x"].rearrange("(b p) f -> p b f", p=P)).then_inc(s_edge, 16)
                e.dma_start(weight[:, :], T["weight_c"]).then_inc(s_edge, 16)
                e.dma_start(iota[:, :], T["iota"].to_broadcast([P, NP_])).then_inc(s_iota, 16)
                e.wait_ge(s_rng, 1)
                e.dma_start(range_dst[0:P, :], small[:, 4:6].bitcast(i32)).then_inc(s_rng_out, 16)
                e.dma_start(range_dst[P:NG, :], small[0:NG - P, 6:8].bitcast(i32)).then_inc(s_rng_out, 16)
                e.wait_ge(s_rng_out, 32)
                e.dma_start(table_dst[:, :], range_dst.rearrange("(a g) c -> a (g c)", a=1)).then_inc(s_rng_in, 16)
                e.wait_ge(s_rng_in, 16)
                e.wait_ge(s_iota, 16)

            @block.scalar
            def _(e):
                e.dma_start(dst_f[:, :].bitcast(i32), T["dst_c"]).then_inc(s_edge, 16)
                e.dma_start(type_f[:, :].bitcast(i32), T["type_c"]).then_inc(s_edge, 16)
                for n in names:
                    to = W[n][:, 0:F]
                    e.dma_start(to, T[n]).then_inc(s_w, 16)
                    n_w[0] += 16
                e.dma_start(attn[:, :], T["attn"]).then_inc(s_w, 16)
                e.dma_start(b1_col[:, :], T["b1_col"]).then_inc(s_w, 16)
                e.dma_start(rel_row[:, :], T["rel_row"].to_broadcast([P, N_RELS])).then_inc(s_w, 16)
                n_w[0] += 48
                for n in bias_names:
                    e.dma_start(bias[n][:, :], T[n].to_broadcast([P, F])).then_inc(s_w, 16)
                    n_w[0] += 16
                e.wait_ge(s_w, n_w[0])

            @block.vector
            def _(e):
                e.wait_ge(s_gd, 32)
                for c, rows_ in ((0, P), (1, NG - P)):
                    e.tensor_reduce(small[0:rows_, 2 * c:2 * c + 1], dst_bc[0:rows_, c, 0:GE], AX, ALU.min)
                    e.tensor_reduce(small[0:rows_, 2 * c + 1:2 * c + 2], dst_bc[0:rows_, c, 0:GE], AX, ALU.max)
                e.drain()
                for c, rows_ in ((0, P), (1, NG - P)):
                    e.tensor_scalar(small[0:rows_, 2 * c + 1:2 * c + 2], small[0:rows_, 2 * c + 1:2 * c + 2],
                                    float(P), None, ALU.add)
                e.drain()
                for c, rows_ in ((0, P), (1, NG - P)):
                    e.tensor_copy(small[0:rows_, 8 + 2 * c:10 + 2 * c].bitcast(i32), small[0:rows_, 2 * c:2 * c + 2])
                e.drain()
                for c, rows_ in ((0, P), (1, NG - P)):
                    ins = e.tensor_scalar(small[0:rows_, 4 + 2 * c:6 + 2 * c].bitcast(i32),
                                          small[0:rows_, 8 + 2 * c:10 + 2 * c].bitcast(i32), 7, None,
                                          ALU.arith_shift_right)
                ins.then_inc(s_rng, 1)
                e.wait_ge(s_edge, 80)
                e.tensor_copy(dst_f[:, :], dst_f[:, :].bitcast(i32))
                e.tensor_copy(type_f[:, :], type_f[:, :].bitcast(i32))
                e.tensor_scalar(pos_i[:, :], src_i[:, :], 7, None, ALU.arith_shift_right)
                e.drain()
                e.tensor_copy(src_block[:, :], pos_i[:, :])
                e.drain()

        def node_products(tag, parts, w_out, finish, store=None):
            s_t, s_tc, s_o, s_f = sem(tag + "_t"), sem(tag + "_tc"), sem(tag + "_o"), sem(tag + "_f")
            k = len(parts)

            def run(block):
                @block.tensor
                def _(e):
                    def transposes(b):
                        if b >= 2:
                            e.wait_ge(s_tc, b - 1)
                        for n, (get, _) in enumerate(parts):
                            ins = e.matmul(bank[b % 2][:, n * P:(n + 1) * P], lhsT=get(b), rhs=ident,
                                           start=True, stop=True)
                        ins.then_inc(s_t, 1)

                    transposes(0)
                    for b in range(NB):
                        if b + 1 < NB:
                            transposes(b + 1)
                        e.wait_ge(s_tc, b + 1)
                        if b >= 2:
                            e.wait_ge(s_f, b - 1)
                        for n, (_, w) in enumerate(parts):
                            ins = e.matmul(bank[2 + b % 2][:, 0:w_out], lhsT=tT[:, b % 2, n * P:(n + 1) * P],
                                           rhs=w[:, 0:w_out], start=(n == 0), stop=(n == k - 1))
                        ins.then_inc(s_o, 1)

                @block.scalar
                def _(e):
                    for b in range(NB):
                        e.wait_ge(s_t, b + 1)
                        if b >= 2:
                            e.wait_ge(s_o, b - 1)
                        e.copy(tT[:, b % 2, 0:k * P], bank[b % 2][:, 0:k * P]).then_inc(s_tc, 1)

                @block.vector
                def _(e):
                    for b in range(NB):
                        e.wait_ge(s_o, b + 1)
                        finish(e, b, bank[2 + b % 2])
                        e.drain().then_inc(s_f, 1)
                    if store:
                        store(e)
            return run

        def layernorm(tag, to):
            s_v, s_sd, s_y, s_st = sem(tag + "_v"), sem(tag + "_sd"), sem(tag + "_y"), sem(tag + "_st")
            with nc.Block() as block:
                @block.vector
                def _(e):
                    for b in range(NB):
                        e.bn_stats(stats[:, :], Xv[:, b, :])
                        e.drain()
                        e.bn_aggr(mv[:, b, :], stats[:, :])
                        e.drain()
                    e.tensor_scalar(rstd[:, :], mv[:, :, 1], EPS, None, ALU.add).then_inc(s_v, 1)
                    e.wait_ge(s_sd, 1)
                    e.reciprocal(rstd[:, :], rstd[:, :])
                    e.drain()
                    for b in range(NB):
                        e.tensor_scalar(Xv[:, b, :], Xv[:, b, :], mv[:, b, 0:1], rstd[:, b:b + 1],
                                        ALU.subtract, ALU.mult)
                    e.drain().then_inc(s_y, 1)

                @block.scalar
                def _(e):
                    e.wait_ge(s_v, 1)
                    e.activation(rstd[:, :], rstd[:, :], ACT.Sqrt).then_inc(s_sd, 1)

                @block.sync
                def _(e):
                    e.wait_ge(s_y, 1)
                    if to is not None:
                        store_nodes(e, to, Xv, s_st)

        def store_nodes(e, to, view, s_st):
            if to is out:
                full = N_NODES // P
                e.dma_start(out[0:full * P, :].rearrange("(b p) f -> p b f", p=P), view[:, 0:full, :]).then_inc(s_st, 16)
                e.dma_start(out[full * P:N_NODES, :], view[0:N_NODES - full * P, full, :]).then_inc(s_st, 16)
                e.wait_ge(s_st, 32)
            else:
                e.dma_start(to.rearrange("(b p) f -> p b f", p=P), view).then_inc(s_st, 16)
                e.wait_ge(s_st, 16)

        def block_range(e, table, g):
            lo = e.value_load(table[0:1, bass.ds(2 * g, 1)], min_val=0, max_val=NB - 1)
            hi = e.value_load(table[0:1, bass.ds(2 * g + 1, 1)], min_val=1, max_val=NB)
            return lo, hi

        def counter(e, name):
            c = e.alloc_register(name)
            e.reg_mov(c, 0)
            return c

        def build_onehot(e, g, b, ids):
            return e.tensor_tensor(
                onehot[:, :, :],
                iota[:, bass.ds(b * P, P)].unsqueeze(1).to_broadcast([P, TILES, P]),
                ids[:, bass.ds(g * TILES, TILES)].unsqueeze(2).to_broadcast([P, TILES, P]), ALU.is_equal)

        def gathers(tag, table, width, s_free):
            s_idx, s_note = sem(tag + "_idx"), sem(tag + "_note")
            s_rows = [sem(f"{tag}_rows{s}") for s in range(SLOTS)]

            def run(block):
                @block.gpsimd
                def _(e):
                    with e.Fori(0, TURNS) as i:
                        for s in range(SLOTS):
                            e.wait_ge(s_free[s], i + 1)
                            e.tensor_copy(idx[:, s, :], src_i[:, bass.ds(i * (SLOTS * TILES) + s * TILES, TILES)]
                                          ).then_inc(s_idx, 1)
                            e.wait_ge(s_idx, i * SLOTS + (s + 1))
                            e.sem_inc(s_note, 1)
                            for t in range(TILES):
                                e.indirect_dma_start(
                                    out=rows[:, s, t, 0:width], out_offset=None, in_=table,
                                    in_offset=bass.IndirectOffsetOnAxis(ap=idx[:, s, t:t + 1], axis=0),
                                ).then_inc(s_rows[s], 16)
            return run, s_rows

        def load_dst_bc(e, s_free_, s_in):
            with e.Fori(0, TURNS) as i:
                for s in range(SLOTS):
                    k = s % 2
                    e.wait_ge(s_free_[k], i * 2 + (s // 2 + 1))
                    e.dma_start(dst_bc[:, k, :], T["dst_row"][bass.ds(i * SLOTS + s, 1), :].to_broadcast([P, GE])
                                ).then_inc(s_in[k], 16)

        s_wa, s_wc, s_zst = sem("l0_wa"), sem("l0_wc"), sem("l0_zst")
        W0 = W["L0_gnn_Wt"]
        with nc.Block() as block:
            @block.tensor
            def _(e):
                e.matmul(bank[7][:, 0:2], lhsT=W["L0_gnn_W"][:, :], rhs=attn[:, :], start=True, stop=True
                         ).then_inc(s_wa, 1)

            @block.vector
            def _(e):
                e.wait_ge(s_wa, 1)
                e.tensor_copy(W0[:, F:ZW], bank[7][:, 0:2]).then_inc(s_wc, 1)
                e.wait_ge(s_wc, 1)
        s_dst_n = sb("s_dst_n", [P, NB])

        def finish_z(e, b, ps):
            e.tensor_copy(A_(ZW)[:, b, :], ps[:, 0:ZW])
            e.tensor_copy(s_dst_n[:, b:b + 1], ps[:, F + 1:F + 2])

        run = node_products("l0z", [(lambda b: Xv[:, b, :], W0)], ZW, finish_z)
        with nc.Block() as block:
            run(block)
        with nc.Block() as block:
            @block.sync
            def _(e):
                store_nodes(e, z_table, A_(ZW), s_zst)

        diag = sb("diag", [P, TILES, P])
        away = sb("away", [P, GE])
        scaled = sb("scaled", [P, TILES, ZW])
        rel_g = sb("rel_g", [P, TILES])
        rel_tmp = sb("rel_tmp", [P, TILES, N_RELS])
        s_max = sb("s_max", [P, NB])
        m_node = sb("m_node", [P, NB])
        q = sb("q", [P, 2])
        e_edge = sb("e_edge", [P, TILES])
        num = sb("num", [P, TILES])
        mscale = sb("mscale", [P, 1])
        s_free = [sem(f"l0_free{s}") for s in range(SLOTS)]
        run_gather, s_rows = gathers("l0g", z_table, ZW, s_free)
        s_bc = [sem(f"l0_bc{k}") for k in range(2)]
        s_bcf = [sem(f"l0_bcf{k}") for k in range(2)]
        s_diag, s_sbc, s_q, s_look, s_ee, s_num, s_w_, s_sc, s_mm, s_nt = (
            sem("l0_" + n) for n in ("diag", "sbc", "q", "look", "ee", "num", "w", "sc", "mm", "nt"))
        A0 = A_(ZW)
        s_src_bc = [bank[0], bank[1]]
        look = bank[2][:, 0:2 * TILES].rearrange("p (t c) -> p t c", c=2)
        with nc.Block() as block:
            run_gather(block)

            @block.sync
            def _(e):
                load_dst_bc(e, s_bcf, s_bc)

            @block.scalar
            def _(e):
                c = counter(e, "l0_act_pairs")
                with e.Fori(0, TURNS) as i:
                    for s in range(SLOTS):
                        g = i * SLOTS + s
                        lo, hi = block_range(e, table_dst, g)
                        e.wait_ge(s_rows[s], (i + 1) * 16 * TILES)
                        e.sem_inc(s_nt, 1)
                        for t in range(TILES):
                            ins = e.activation(diag[:, t, :], ident, ACT.Copy, scale=rows[:, s, t, F:F + 1])
                        ins.then_inc(s_diag, 1)
                        with e.Fori(lo, hi):
                            e.reg_add(c, c, 1)
                            e.wait_ge(s_ee, c)
                            e.activation(num[:, :], e_edge[:, :], ACT.Exp)
                            e.activation(mscale[:, :], mscale[:, :], ACT.Exp).then_inc(s_num, 1)
                            e.wait_ge(s_w_, c)
                            for t in range(TILES):
                                ins = e.activation(scaled[:, t, 0:F], rows[:, s, t, 0:F], ACT.Copy,
                                                   scale=e_edge[:, t:t + 1])
                            ins.then_inc(s_sc, 1)
                        e.drain().then_inc(s_free[s], 1)

            @block.tensor
            def _(e):
                c = counter(e, "l0_pe_pairs")
                with e.Fori(0, NG) as g:
                    lo, hi = block_range(e, table_dst, g)
                    e.wait_ge(s_diag, g + 1)
                    for h in range(2):
                        ins = e.matmul(s_src_bc[h][:, :], lhsT=ones, rhs=diag[:, 4 * h:4 * h + 4, :].rearrange(
                            "p t n -> p (t n)"), start=True, stop=True)
                    ins.then_inc(s_sbc, 1)
                    with e.Fori(lo, hi):
                        e.reg_add(c, c, 1)
                        e.wait_ge(s_q, c)
                        for t in range(TILES):
                            ins = e.matmul(look[:, t, :], lhsT=onehot_t[:, t * P:(t + 1) * P], rhs=q[:, :],
                                           start=True, stop=True)
                        ins.then_inc(s_look, 1)
                        e.wait_ge(s_sc, c)
                        for t in range(TILES):
                            ins = e.matmul(bank[3][:, 0:ZW], lhsT=onehot[:, t, :], rhs=scaled[:, t, :],
                                           start=(t == 0), stop=(t == TILES - 1))
                        ins.then_inc(s_mm, 1)

            @block.vector
            def _(e):
                c = counter(e, "l0_dve_pairs")
                e.memset(A[:, :], 0.0)
                e.memset(s_max[:, :], -HUGE)
                e.memset(m_node[:, :], -HUGE * SLOPE)
                e.memset(scaled[:, :, :], 1.0)
                e.drain()
                for s in range(SLOTS):
                    e.sem_inc(s_free[s], 1)
                for k in range(2):
                    e.sem_inc(s_bcf[k], 1)
                with e.Fori(0, TURNS) as i:
                    for s in range(SLOTS):
                        g, k = i * SLOTS + s, s % 2
                        lo, hi = block_range(e, table_dst, g)
                        e.tensor_tensor(rel_tmp[:, :, :], iota[:, 0:N_RELS].unsqueeze(1).to_broadcast([P, TILES, N_RELS]),
                                        type_f[:, bass.ds(g * TILES, TILES)].unsqueeze(2).to_broadcast([P, TILES, N_RELS]),
                                        ALU.is_equal)
                        e.drain()
                        e.tensor_tensor(rel_tmp[:, :, :], rel_tmp[:, :, :],
                                        rel_row[:, :].unsqueeze(1).to_broadcast([P, TILES, N_RELS]), ALU.mult)
                        e.drain()
                        e.tensor_reduce(rel_g[:, :], rel_tmp[:, :, :], AX, ALU.add)
                        e.wait_ge(s_bc[k], (i * 2 + (s // 2 + 1)) * 16)
                        e.sem_inc(s_nt, 1)
                        with e.Fori(lo, hi) as b:
                            e.reg_add(c, c, 1)
                            nid = node_id[:, bass.ds(b, 1)]
                            e.tensor_scalar(onehot_t[:, :], dst_bc[:, k, :], nid, None, ALU.is_equal)
                            e.tensor_scalar(away[:, :], dst_bc[:, k, :], nid, -HUGE, ALU.not_equal, ALU.mult)
                            build_onehot(e, g, b, dst_f)
                            e.drain()
                            e.wait_ge(s_sbc, g + 1)
                            e.sem_inc(s_nt, 1)
                            for h in range(2):
                                e.tensor_tensor_reduce(out=away[:, h * 512:(h + 1) * 512], in0=s_src_bc[h][:, :],
                                                       in1=away[:, h * 512:(h + 1) * 512], scale=1.0, scalar=-HUGE,
                                                       op0=ALU.add, op1=ALU.max, accum_out=small[:, 16 + h:17 + h])
                            e.drain()
                            e.tensor_tensor(small[:, 18:19], small[:, 16:17], small[:, 17:18], ALU.max)
                            e.drain()
                            e.tensor_tensor(s_max[:, bass.ds(b, 1)], s_max[:, bass.ds(b, 1)], small[:, 18:19], ALU.max)
                            e.tensor_copy(q[:, 0:1], s_dst_n[:, bass.ds(b, 1)])
                            e.drain()
                            e.tensor_tensor(small[:, 19:20], s_max[:, bass.ds(b, 1)], q[:, 0:1], ALU.add)
                            e.drain()
                            e.scalar_tensor_tensor(out=q[:, 1:2], in0=small[:, 19:20], scalar=SLOPE, in1=small[:, 19:20],
                                                   op0=ALU.mult, op1=ALU.max)
                            e.drain().then_inc(s_q, 1)
                            e.tensor_tensor(mscale[:, :], m_node[:, bass.ds(b, 1)], q[:, 1:2], ALU.subtract)
                            e.wait_ge(s_look, c)
                            e.tensor_tensor(e_edge[:, :], rows[:, s, :, F], look[:, :, 0], ALU.add)
                            e.drain()
                            e.tensor_copy(m_node[:, bass.ds(b, 1)], q[:, 1:2])
                            e.scalar_tensor_tensor(out=num[:, :], in0=e_edge[:, :], scalar=SLOPE, in1=e_edge[:, :],
                                                   op0=ALU.mult, op1=ALU.max)
                            e.drain()
                            e.tensor_tensor(e_edge[:, :], num[:, :], look[:, :, 1], ALU.subtract)
                            e.drain()
                            e.tensor_scalar(e_edge[:, :], e_edge[:, :], 0.0, None, ALU.min)
                            e.drain().then_inc(s_ee, 1)
                            e.wait_ge(s_num, c)
                            e.tensor_copy(scaled[:, :, F], num[:, :])
                            e.tensor_tensor(e_edge[:, :], num[:, :], rel_g[:, :], ALU.mult)
                            e.drain().then_inc(s_w_, 1)
                            e.wait_ge(s_mm, c)
                            e.scalar_tensor_tensor(out=A[:, bass.ds(b * ZW, F + 1)], in0=A[:, bass.ds(b * ZW, F + 1)],
                                                   scalar=mscale[:, 0:1], in1=bank[3][:, 0:F + 1],
                                                   op0=ALU.mult, op1=ALU.add)
                            e.tensor_tensor(A[:, bass.ds(b * ZW + F + 1, 1)], A[:, bass.ds(b * ZW + F + 1, 1)],
                                            bank[3][:, F + 1:F + 2], ALU.add)
                            e.drain()
                        e.drain().then_inc(s_bcf[k], 1)

        rden = sb("rden", [P, NB])
        deg_r = sb("deg_r", [P, NB])
        with nc.Block() as block:
            @block.vector
            def _(e):
                e.tensor_scalar(rden[:, :], A0[:, :, F], TINY, None, ALU.max)
                e.tensor_scalar(deg_r[:, :], A0[:, :, F + 1], 1.0, None, ALU.max)
                e.drain()
                e.reciprocal(rden[:, :], rden[:, :])
                e.reciprocal(deg_r[:, :], deg_r[:, :])
                e.drain()
                for b in range(NB):
                    e.scalar_tensor_tensor(out=Xv[:, b, :], in0=A0[:, b, 0:F], scalar=rden[:, b:b + 1],
                                           in1=Xv[:, b, :], op0=ALU.mult, op1=ALU.add)
                e.drain()
                e.tensor_tensor(Xv, Xv, bias["L0_gnn_bias_w"][:, :].unsqueeze(1).to_broadcast([P, NB, F]), ALU.add)
                e.drain()
        layernorm("l0n", x_tables[0])
        release_semaphores()

        A1 = A_(F)

        def sum_pass(tag, table, weighted, extra):
            s_free = [sem(f"{tag}_free{s}") for s in range(SLOTS)]
            run_gather, s_rows = gathers(tag, table, F, s_free)
            s_ready = [sem(f"{tag}_ready{s}") for s in range(SLOTS)]
            s_oh, s_mm, s_note_a = sem(tag + "_oh"), sem(tag + "_mm"), sem(tag + "_note_a")
            with nc.Block() as block:
                run_gather(block)
                if weighted:
                    @block.scalar
                    def _(e):
                        with e.Fori(0, TURNS) as i:
                            for s in range(SLOTS):
                                e.wait_ge(s_rows[s], (i + 1) * 16 * TILES)
                                e.sem_inc(s_note_a, 1)
                                for t in range(TILES):
                                    e.activation(rows[:, s, t, 0:F], rows[:, s, t, 0:F], ACT.Copy,
                                                 scale=weight[:, bass.ds(i * (SLOTS * TILES) + (s * TILES + t), 1)])
                                e.drain().then_inc(s_ready[s], 1)

                @block.tensor
                def _(e):
                    c = counter(e, tag + "_pe_pairs")
                    for s in range(SLOTS):
                        e.sem_inc(s_free[s], 1)
                    with e.Fori(0, TURNS) as i:
                        for s in range(SLOTS):
                            lo, hi = block_range(e, table_dst, i * SLOTS + s)
                            if weighted:
                                e.wait_ge(s_ready[s], i + 1)
                            else:
                                e.wait_ge(s_rows[s], (i + 1) * 16 * TILES)
                            e.sem_inc(s_note_a, 1)
                            with e.Fori(lo, hi):
                                e.reg_add(c, c, 1)
                                e.wait_ge(s_oh, c)
                                for t in range(TILES):
                                    ins = e.matmul(bank[3][:, 0:F], lhsT=onehot[:, t, :], rhs=rows[:, s, t, 0:F],
                                                   start=(t == 0), stop=(t == TILES - 1))
                                ins.then_inc(s_mm, 1)
                            e.drain().then_inc(s_free[s], 1)

                @block.vector
                def _(e):
                    c = counter(e, tag + "_dve_pairs")
                    e.memset(A[:, 0:NB * F], 0.0)
                    e.drain()
                    with e.Fori(0, TURNS) as i:
                        if extra:
                            extra(e, i)
                        for s in range(SLOTS):
                            g = i * SLOTS + s
                            lo, hi = block_range(e, table_dst, g)
                            with e.Fori(lo, hi) as b:
                                e.reg_add(c, c, 1)
                                build_onehot(e, g, b, dst_f)
                                e.drain().then_inc(s_oh, 1)
                                e.wait_ge(s_mm, c)
                                e.tensor_tensor(A[:, bass.ds(b * F, F)], A[:, bass.ds(b * F, F)], bank[3][:, 0:F],
                                                ALU.add)
                                e.drain()


        def count_bucket(e, i):
            e.tensor_scalar(mask[:, :], src_block[:, :], iota[:, bass.ds(i, 1)], None, ALU.is_equal)
            e.drain()
            e.tensor_reduce(tot[:, bass.ds(i, 1)], mask[:, :], AX, ALU.add)

        def place_bucket(e, i):
            e.tensor_scalar(mask[:, :], src_block[:, :], iota[:, bass.ds(i, 1)], None, ALU.is_equal)
            e.tensor_copy(small[:, 20:21], base[:, bass.ds(i, 1)])
            e.drain()
            e.tensor_tensor_scan(cum[:, :], mask[:, :], mask[:, :], small[:, 20:21], ALU.add, ALU.max)
            e.drain()
            e.copy_predicated(pos[:, :], mask[:, :].bitcast(u32), cum[:, :])
            e.drain()

        sum_pass("l1", x_tables[0], False, count_bucket)

        s_tot, s_ps, s_base, s_ro, s_ri = sem("so_tot"), sem("so_ps"), sem("so_base"), sem("so_ro"), sem("so_ri")
        with nc.Block() as block:
            @block.tensor
            def _(e):
                e.matmul(bank[4][:, 0:NB], lhsT=tri, rhs=tot[:, :], start=True, stop=True)
                e.matmul(bank[5][:, 0:NB], lhsT=ones, rhs=tot[:, :], start=True, stop=True).then_inc(s_ps, 1)

            @block.vector
            def _(e):
                e.wait_ge(s_ps, 1)
                e.tensor_copy(tot[:, :], bank[5][:, 0:NB])
                e.drain()
                e.tensor_tensor_scan(end_of[:, :], tot[:, :], tot[:, :], 0.0, ALU.add, ALU.max)
                e.drain()
                e.tensor_tensor(start_of[:, :], end_of[:, :], bank[5][:, 0:NB], ALU.subtract)
                e.drain()
                e.tensor_tensor(base[:, :], start_of[:, :], bank[4][:, 0:NB], ALU.add)
                for c in range(2):
                    e.tensor_scalar(cum[:, 0:NB], end_of[:, :], group_at[:, c:c + 1], None, ALU.is_le)
                    e.tensor_scalar(mask[:, 0:NB], start_of[:, :], group_at[:, c:c + 1], float(GE - 1),
                                    ALU.subtract, ALU.is_le)
                    e.drain()
                    e.tensor_reduce(small[:, 24 + 2 * c:25 + 2 * c], cum[:, 0:NB], AX, ALU.add)
                    e.tensor_reduce(small[:, 25 + 2 * c:26 + 2 * c], mask[:, 0:NB], AX, ALU.add)
                    e.drain()
                    ins = e.tensor_copy(small[:, 28 + 2 * c:30 + 2 * c].bitcast(i32), small[:, 24 + 2 * c:26 + 2 * c])
                    e.drain()
                e.drain().then_inc(s_base, 1)

            @block.sync
            def _(e):
                e.wait_ge(s_base, 1)
                for c in range(2):
                    e.dma_start(range_src[c * HG:(c + 1) * HG, :], small[0:HG, 28 + 2 * c:30 + 2 * c].bitcast(i32)
                                ).then_inc(s_ro, 16)
                e.wait_ge(s_ro, 32)
                e.dma_start(table_src[:, :], range_src.rearrange("(a g) c -> a (g c)", a=1)).then_inc(s_ri, 16)
                e.wait_ge(s_ri, 16)

        with nc.Block() as block:
            @block.vector
            def _(e):
                for b in range(NB):
                    e.tensor_scalar(A1[:, b, :], A1[:, b, :], deg_r[:, b:b + 1], None, ALU.mult)
                e.drain()

        def add_to_x(e, b, ps):
            e.tensor_tensor(Xv[:, b, :], Xv[:, b, :], ps[:, 0:F], ALU.add)

        run = node_products("l1d", [(lambda b: A1[:, b, :], W["L1_gnn_W_lt"]), (lambda b: Xv[:, b, :], W["L1_gnn_W_rt"])],
                            F, add_to_x)
        with nc.Block() as block:
            run(block)
        layernorm("l1n", x_tables[1])
        release_semaphores()

        Hv = H[:, :].rearrange("p (b f) -> p b f", f=F)
        for k in range(3):
            sum_pass(f"l2{k}", x_tables[1 + k] if k < 2 else x_tables[3], True, place_bucket if k == 0 else None)
            b_row = bias[f"L2_gnn_b_rel{k + 1}"]

            def finish_conv(e, b, ps, k=k, b_row=b_row):
                if k < 2:
                    e.tensor_tensor(Hv[:, b, :], ps[:, 0:F], b_row[:, :], ALU.add)
                    e.drain()
                    e.tensor_scalar(Hv[:, b, :], Hv[:, b, :], 0.0, None, ALU.max)
                else:
                    e.tensor_tensor(Xv[:, b, :], Xv[:, b, :], ps[:, 0:F], ALU.add)
                    e.drain()
                    e.tensor_tensor(Xv[:, b, :], Xv[:, b, :], b_row[:, :], ALU.add)

            own = Xv if k == 0 else Hv
            run = node_products(f"l2d{k}", [(lambda b: A1[:, b, :], W[f"L2_gnn_W_rel{k + 1}t"]),
                                            (lambda b, own=own: own[:, b, :], W[f"L2_gnn_W_root{k + 1}t"])],
                                F, finish_conv)
            with nc.Block() as block:
                run(block)
            if k < 2:
                s_hst = sem(f"l2_hst{k}")
                with nc.Block() as block:
                    @block.sync
                    def _(e):
                        store_nodes(e, x_tables[2 + k], Hv, s_hst)
        layernorm("l2n", None)
        release_semaphores()

        def finish_h(e, b, ps):
            e.tensor_tensor(Hv[:, b, :], ps[:, 0:F], bias["L3_gnn_bl"][:, :], ALU.add)

        s_pos = sem("s_pos")
        run = node_products("l3h", [(lambda b: Xv[:, b, :], W["L3_gnn_Wl"])], F, finish_h)
        with nc.Block() as block:
            run(block)

            @block.gpsimd
            def _(e):
                e.tensor_scalar(pos[:, :], pos[:, :], -1.0, None, ALU.add).then_inc(s_pos, 1)
                e.wait_ge(s_pos, 1)
                e.tensor_copy(pos_i[:, :], pos[:, :]).then_inc(s_pos, 1)
                e.wait_ge(s_pos, 2)

        attr = onehot[:, :, :].rearrange("p (k t) n -> p k (t n)", k=2)
        hid = diag[:, :, :].rearrange("p t n -> p (t n)")
        h_edge = away
        s_bc = [sem(f"l3_bc{k}") for k in range(2)]
        s_bcf = [sem(f"l3_bcf{k}") for k in range(2)]
        s_at = [sem(f"l3_at{k}") for k in range(2)]
        s_atf = [sem(f"l3_atf{k}") for k in range(2)]
        s_msg, s_mm1, s_hid, s_mm2, s_wf, s_ot, s_g, s_idx, s_nt = (
            sem("l3_" + n) for n in ("msg", "mm1", "hid", "mm2", "wf", "ot", "g", "idx", "nt"))
        s_scat = [sem(f"l3_scat{s}") for s in range(SLOTS)]
        with nc.Block() as block:
            @block.sync
            def _(e):
                with e.Fori(0, TURNS) as i:
                    for s in range(SLOTS):
                        k = s % 2
                        e.wait_ge(s_bcf[k], i * 2 + (s // 2 + 1))
                        e.dma_start(dst_bc[:, k, :], T["dst_row"][bass.ds(i * SLOTS + s, 1), :].to_broadcast([P, GE])
                                    ).then_inc(s_bc[k], 16)
                        e.wait_ge(s_atf[k], i * 2 + (s // 2 + 1))
                        e.dma_start(attr[:, k, :], T["attr_t"][bass.ds(i * SLOTS + s, 1), :, :].rearrange(
                            "a p n -> (a p) n")).then_inc(s_at[k], 16)

            @block.tensor
            def _(e):
                c = counter(e, "l3_pe_pairs")
                for k in range(2):
                    e.sem_inc(s_atf[k], 1)
                with e.Fori(0, TURNS) as i:
                    for s in range(SLOTS):
                        g, k = i * SLOTS + s, s % 2
                        lo, hi = block_range(e, table_dst, g)
                        e.wait_ge(s_at[k], (i * 2 + (s // 2 + 1)) * 16)
                        e.sem_inc(s_nt, 1)
                        for h in range(2):
                            r = slice(h * N_RBF, (h + 1) * N_RBF)
                            ins = e.matmul(bank[h][:, :], lhsT=W["L3_gnn_W1d"][r, 0:F], rhs=attr[r, k, :],
                                           start=True, stop=True)
                        ins.then_inc(s_mm1, 1)
                        e.wait_ge(s_hid, g + 1)
                        e.sem_inc(s_nt, 1)
                        e.drain().then_inc(s_atf[k], 1)
                        e.wait_ge(s_wf, g + 1)
                        e.sem_inc(s_nt, 1)
                        for t in range(TILES):
                            ins = e.matmul(bank[2 + t // 4][:, (t % 4) * P:(t % 4 + 1) * P],
                                           lhsT=hid[:, t * P:(t + 1) * P], rhs=W["L3_gnn_W2"][:, :],
                                           start=True, stop=True)
                        ins.then_inc(s_mm2, 1)
                        with e.Fori(lo, hi) as b:
                            e.reg_add(c, c, 1)
                            e.wait_ge(s_ot, c)
                            e.sem_inc(s_nt, 1)
                            for t in range(TILES):
                                ins = e.matmul(bank[4 + t // 4][:, (t % 4) * P:(t % 4 + 1) * P],
                                               lhsT=onehot_t[:, t * P:(t + 1) * P], rhs=H[:, bass.ds(b * F, F)],
                                               start=True, stop=True)
                            ins.then_inc(s_g, 1)

            @block.scalar
            def _(e):
                with e.Fori(0, NG) as g:
                    e.wait_ge(s_mm1, g + 1)
                    for h in range(2):
                        ins = e.activation(hid[:, h * 512:(h + 1) * 512], bank[h][:, :], ACT.Relu, bias=b1_col[:, 0:1])
                    ins.then_inc(s_hid, 1)

            @block.vector
            def _(e):
                c = counter(e, "l3_dve_pairs")
                for k in range(2):
                    e.sem_inc(s_bcf[k], 1)
                e.sem_inc(s_wf, 1)
                with e.Fori(0, TURNS) as i:
                    for s in range(SLOTS):
                        g, k = i * SLOTS + s, s % 2
                        lo, hi = block_range(e, table_dst, g)
                        e.memset(h_edge[:, :], 0.0)
                        e.wait_ge(s_bc[k], (i * 2 + (s // 2 + 1)) * 16)
                        e.sem_inc(s_nt, 1)
                        with e.Fori(lo, hi) as b:
                            e.reg_add(c, c, 1)
                            e.tensor_scalar(onehot_t[:, :], dst_bc[:, k, :], node_id[:, bass.ds(b, 1)], None, ALU.is_equal)
                            e.drain().then_inc(s_ot, 1)
                            e.wait_ge(s_g, c)
                            for h in range(2):
                                r = slice(h * 512, (h + 1) * 512)
                                e.tensor_tensor(h_edge[:, r], h_edge[:, r], bank[4 + h][:, :], ALU.add)
                            e.drain()
                        e.drain().then_inc(s_bcf[k], 1)
                        with e.If(i > 0):
                            e.wait_ge(s_scat[s], i * (16 * TILES))
                            e.sem_inc(s_nt, 1)
                        e.wait_ge(s_mm2, g + 1)
                        for h in range(2):
                            e.tensor_tensor(rows[:, s, 4 * h:4 * h + 4, 0:F],
                                            bank[2 + h][:, :].rearrange("p (t f) -> p t f", f=F),
                                            bias["L3_gnn_b2"][:, :].unsqueeze(1).to_broadcast([P, 4, F]), ALU.add)
                        e.tensor_copy(rows[:, s, :, F], src_i[:, bass.ds(g * TILES, TILES)])
                        e.drain().then_inc(s_wf, 1)
                        e.tensor_tensor(rows[:, s, :, 0:F], rows[:, s, :, 0:F],
                                        h_edge[:, :].rearrange("p (t f) -> p t f", f=F), ALU.mult)
                        e.drain().then_inc(s_msg, 1)

            @block.gpsimd
            def _(e):
                with e.Fori(0, TURNS) as i:
                    for s in range(SLOTS):
                        e.wait_ge(s_msg, i * SLOTS + (s + 1))
                        e.tensor_copy(idx[:, s, :], pos_i[:, bass.ds(i * (SLOTS * TILES) + s * TILES, TILES)]
                                      ).then_inc(s_idx, 1)
                        e.wait_ge(s_idx, i * SLOTS + (s + 1))
                        e.sem_inc(s_nt, 1)
                        for t in range(TILES):
                            e.indirect_dma_start(
                                out=sorted_rows, out_offset=bass.IndirectOffsetOnAxis(ap=idx[:, s, t:t + 1], axis=0),
                                in_=rows[:, s, t, 0:MW], in_offset=None).then_inc(s_scat[s], 16)
                for s in range(SLOTS):
                    e.wait_ge(s_scat[s], TURNS * 16 * TILES)

        s_in = [sem(f"l3_in{s}") for s in range(SLOTS)]
        s_inf = [sem(f"l3_inf{s}") for s in range(SLOTS)]
        s_oh, s_mm = sem("l3_oh"), sem("l3_mm")
        msgs = [rows[:, s, :, :].rearrange("p t w -> p (t w)")[:, 0:TILES * MW] for s in range(SLOTS)]
        sorted_v = sorted_rows.rearrange("(g p t) w -> g p (t w)", p=P, t=TILES)
        with nc.Block() as block:
            @block.sync
            def _(e):
                with e.Fori(0, TURNS) as i:
                    for s in range(SLOTS):
                        e.wait_ge(s_inf[s], i + 1)
                        e.dma_start(msgs[s], sorted_v[bass.ds(i * SLOTS + s, 1), :, :].rearrange("a p n -> (a p) n")
                                    ).then_inc(s_in[s], 16)

            @block.tensor
            def _(e):
                c = counter(e, "l3b_pe_pairs")
                for s in range(SLOTS):
                    e.sem_inc(s_inf[s], 1)
                with e.Fori(0, TURNS) as i:
                    for s in range(SLOTS):
                        lo, hi = block_range(e, table_src, i * SLOTS + s)
                        e.wait_ge(s_in[s], (i + 1) * 16)
                        e.sem_inc(s_nt, 1)
                        mv_ = msgs[s].rearrange("p (t w) -> p t w", w=MW)
                        with e.Fori(lo, hi):
                            e.reg_add(c, c, 1)
                            e.wait_ge(s_oh, c)
                            for t in range(TILES):
                                ins = e.matmul(bank[3][:, 0:F], lhsT=onehot[:, t, :], rhs=mv_[:, t, 0:F],
                                               start=(t == 0), stop=(t == TILES - 1))
                            ins.then_inc(s_mm, 1)
                        e.drain().then_inc(s_inf[s], 1)

            @block.vector
            def _(e):
                c = counter(e, "l3b_dve_pairs")
                e.memset(A[:, 0:NB * F], 0.0)
                e.drain()
                with e.Fori(0, TURNS) as i:
                    for s in range(SLOTS):
                        lo, hi = block_range(e, table_src, i * SLOTS + s)
                        e.wait_ge(s_in[s], (i + 1) * 16)
                        e.sem_inc(s_nt, 1)
                        mv_ = msgs[s].rearrange("p (t w) -> p t w", w=MW)
                        with e.Fori(lo, hi) as b:
                            e.reg_add(c, c, 1)
                            e.tensor_tensor(onehot[:, :, :],
                                            iota[:, bass.ds(b * P, P)].unsqueeze(1).to_broadcast([P, TILES, P]),
                                            mv_[:, :, F:F + 1].to_broadcast([P, TILES, P]), ALU.is_equal)
                            e.drain().then_inc(s_oh, 1)
                            e.wait_ge(s_mm, c)
                            e.tensor_tensor(A[:, bass.ds(b * F, F)], A[:, bass.ds(b * F, F)], bank[3][:, 0:F], ALU.add)
                            e.drain()
                e.tensor_tensor(X[:, :], X[:, :], A[:, 0:NB * F], ALU.add)
                e.drain()
        layernorm("l3n", out)


def kernel(**inputs):
    import numpy as np
    from concourse import bacc
    from concourse.bass_utils import run_bass_kernel_spmd

    a = {n: np.ascontiguousarray(np.asarray(v)) for n, v in inputs.items()}

    def padded(v, n, fill):
        o = np.full((n,) + v.shape[1:], fill, v.dtype)
        o[:v.shape[0]] = v
        return o

    def columns(v):
        return np.ascontiguousarray(v.reshape(NG, P, TILES).transpose(1, 0, 2).reshape(P, NG * TILES))

    dst = padded(a["dst"], EP, PAD_NODE)
    attr = padded(a["edge_attr_64"], EP, 0).reshape(NG, P, TILES, N_RBF)
    attr_t = np.ascontiguousarray(attr.transpose(0, 2, 3, 1).reshape(NG, 2, TILES // 2, N_RBF, P)
                                  .transpose(0, 1, 3, 2, 4).reshape(NG, 2 * N_RBF, GE // 2))
    consts = np.zeros((P, C_WIDTH), np.float32)
    consts[:, C_IDENT:C_IDENT + P] = np.eye(P)
    consts[:, C_TRI:C_TRI + P] = np.triu(np.ones((P, P)), 1)
    consts[:, C_ONES:C_ONES + P] = 1.0
    consts[:, C_NODE:C_NODE + NB] = np.arange(P)[:, None] + P * np.arange(NB)[None, :]
    consts[:, C_GROUP:C_GROUP + 2] = GE * (np.arange(P)[:, None] + HG * np.arange(2)[None, :])
    feeds = {
        "x": padded(a["x"], NP_, 0),
        "src_c": columns(padded(a["src"], EP, PAD_NODE)),
        "dst_c": columns(dst),
        "type_c": columns(padded(a["edge_type_40"], EP, 0)),
        "weight_c": columns(padded(a["edge_weight"], EP, 0)),
        "dst_row": np.ascontiguousarray(dst.reshape(NG, P, TILES).transpose(0, 2, 1).reshape(NG, GE)),
        "attr_t": attr_t,
        "consts": consts,
        "iota": np.arange(NP_, dtype=np.float32)[None, :],
        "L0_gnn_W": a["L0_gnn_W"],
        "L0_gnn_Wt": np.ascontiguousarray(a["L0_gnn_W"].T),
        "attn": np.ascontiguousarray(a["L0_gnn_attn_w"].reshape(2, F).T),
        "rel_row": a["L0_gnn_rel_emb"].reshape(1, N_RELS),
        "b1_col": a["L3_gnn_b1"].reshape(P, 1),
        "L3_gnn_W1d": np.concatenate([a["L3_gnn_W1"]] * 2, axis=0),
        "L3_gnn_W2": a["L3_gnn_W2"],
        "L3_gnn_Wl": a["L3_gnn_Wl"],
    }
    for n in ("L1_gnn_W_l", "L1_gnn_W_r", "L2_gnn_W_rel1", "L2_gnn_W_root1", "L2_gnn_W_rel2", "L2_gnn_W_root2",
              "L2_gnn_W_rel3", "L2_gnn_W_root3"):
        feeds[n + "t"] = np.ascontiguousarray(a[n].T)
    for n in ("L0_gnn_bias_w", "L2_gnn_b_rel1", "L2_gnn_b_rel2", "L2_gnn_b_rel3", "L3_gnn_b2", "L3_gnn_bl"):
        feeds[n] = a[n].reshape(1, F)

    nc = bacc.Bacc("TRN2", target_bir_lowering=False, num_devices=1)
    T = {n: nc.dram_tensor("in_" + n, v.shape, mybir.dt.from_np(v.dtype), kind="ExternalInput").ap()
         for n, v in feeds.items()}
    out = nc.dram_tensor("out_0", (N_NODES, F), f32, kind="ExternalOutput").ap()
    build_program(nc, T, out)
    r = run_bass_kernel_spmd(nc, [{"in_" + n: v for n, v in feeds.items()}], core_ids=[0])
    return r.results[0]["out_0"]
```

```python
from contextlib import ExitStack

import concourse.bass as bass
import concourse.mybir as mybir
from concourse.alu_op_type import AluOpType as ALU

P = 128
F = 128
N_NODES = 6250
N_EDGES = 200000
N_RELS = 40
N_RBF = 64
NB = -(-N_NODES // P)
NP_ = NB * P
TILES = 8
GE = TILES * P
NG = -(-N_EDGES // GE)
EP = NG * GE
SLOTS = 4
TURNS = NG // SLOTS
PAD_NODE = NP_ - 1
assert NG % SLOTS == 0 and TURNS == NB and PAD_NODE >= N_NODES
HG = NG // 2
ZW = F + 4
S_SRC, S_DST, S_PARTS = F, F + 1, 2 * (F + 2)
PARTS = 4
MW = F + 1
HUGE = 3.0e38
TINY = 1.0e-30
EPS = 1.0e-5
SLOPE = 0.01
C_IDENT, C_TRI, C_ONES, C_NODE, C_GROUP = 0, P, 2 * P, 3 * P, 3 * P + NB
C_SPREAD = C_GROUP + 2
C_WIDTH = C_SPREAD + GE
FAR = 2.0 ** 51

f32 = mybir.dt.float32
bf16 = mybir.dt.bfloat16
i32 = mybir.dt.int32
u32 = mybir.dt.uint32
AX = mybir.AxisListType.X
ACT = mybir.ActivationFunctionType


def build_program(nc, T, out):
    ctx = ExitStack()
    with ctx:
        def sb(name, shape, dt=f32):
            return ctx.enter_context(nc.sbuf_tensor(name, shape, dt))

        live = []

        def sem(name):
            live.append(nc.alloc_semaphore(name=name))
            return live[-1]

        def release_semaphores():
            with nc.Block() as block:
                @block.gpsimd
                def _(e):
                    nc.clear_and_free_semaphores(list(live))
                    e.drain()
            live.clear()

        def dram(name, shape, dt=f32):
            return nc.dram_tensor(name, shape, dt, kind="Internal").ap()

        consts = sb("consts", [P, C_SPREAD])
        ident = consts[:, C_IDENT:C_IDENT + P]
        tri = consts[:, C_TRI:C_TRI + P]
        ones = consts[:, C_ONES:C_ONES + P]
        node_id = consts[:, C_NODE:C_NODE + NB]
        group_at = consts[:, C_GROUP:C_GROUP + 2]
        spread = sb("spread", [PARTS * TILES, GE], bf16)
        ident_h = sb("ident_h", [P, P], bf16)
        iota = sb("iota", [P, NP_])
        names = ["L0_gnn_W", "L0_gnn_Wt", "L1_gnn_W_lt", "L1_gnn_W_rt", "L2_gnn_W_rel1t", "L2_gnn_W_root1t",
                 "L2_gnn_W_rel2t", "L2_gnn_W_root2t", "L2_gnn_W_rel3t", "L2_gnn_W_root3t",
                 "L3_gnn_W1d", "L3_gnn_W2", "L3_gnn_Wl"]
        W = {n: sb("w_" + n, [P, F + 2 if n == "L0_gnn_Wt" else F]) for n in names}
        attn = sb("attn", [P, 2])
        bias_names = ["L0_gnn_bias_w", "L2_gnn_b_rel1", "L2_gnn_b_rel2", "L2_gnn_b_rel3", "L3_gnn_b2", "L3_gnn_bl"]
        bias = {n: sb("b_" + n, [P, F]) for n in bias_names}
        b1_col = sb("b1_col", [P, 1])
        rel_row = sb("rel_row", [P, N_RELS])
        src_i = sb("src_i", [P, NG * TILES], i32)
        dst_f = sb("dst_f", [P, NG * TILES])
        type_f = sb("type_f", [P, NG * TILES])
        weight = sb("weight", [P, NG * TILES])
        pos = type_f
        pos_i = sb("pos_i", [P, NG * TILES], i32)
        X = sb("X", [P, NB * F])
        A = sb("A", [P, NB * ZW])
        H = sb("H", [P, NB * F])
        src_block, mask, cum, rel = (H[:, k * NG * TILES:(k + 1) * NG * TILES] for k in range(4))
        rows = sb("rows", [P, SLOTS, TILES, ZW])
        idx = sb("idx", [P, SLOTS, TILES], i32)
        onehot = sb("onehot", [P, TILES, P])
        onehot_t = sb("onehot_t", [P, GE])
        dst_bc = sb("dst_bc", [P, 2, GE], i32)
        table_dst = sb("table_dst", [1, 2 * NG], i32)
        table_src = sb("table_src", [1, 2 * NG], i32)
        small = sb("small", [P, 64])
        tot = sb("tot", [P, NB])
        base = sb("base", [P, NB])
        start_of = sb("start_of", [P, NB])
        end_of = sb("end_of", [P, NB])
        stats = sb("stats", [P, 6])
        mv = sb("mv", [P, NB, 2])
        rstd = sb("rstd", [P, NB])
        tT = sb("tT", [P, 2, 2 * P])
        one_f = sb("one_f", [P, 1])
        one_col = sb("one_col", [P, 1], bf16)
        wide = ctx.enter_context(nc.psum_tensor("wide", [P, GE], f32))
        bank = [None, None] + [ctx.enter_context(nc.psum_tensor(f"bank{k}", [P, 512], f32)) for k in range(2, 8)]

        def A_(w):
            return A[:, 0:NB * w].rearrange("p (b f) -> p b f", f=w)

        Xv = X[:, :].rearrange("p (b f) -> p b f", f=F)
        z_table = dram("z_table", (NP_, ZW))
        x_tables = [dram(f"x_table{k}", (NP_, F)) for k in range(4)]
        sorted_rows = dram("sorted_rows", (EP, MW))
        range_dst = dram("range_dst", (NG, 2), i32)
        range_src = dram("range_src", (NG, 2), i32)

        s_small, s_edge, s_iota, s_w = sem("s_small"), sem("s_edge"), sem("s_iota"), sem("s_w")
        s_gd, s_rng, s_rng_out, s_rng_in = sem("s_gd"), sem("s_rng"), sem("s_rng_out"), sem("s_rng_in")
        n_w = [0]
        gd = onehot[:, :, :].rearrange("p a b -> p (a b)").bitcast(i32)
        with nc.Block() as block:
            @block.sync
            def _(e):
                e.dma_start(consts[:, :], T["consts"][:, 0:C_SPREAD]).then_inc(s_small, 16)
                e.dma_start(onehot_t[0:PARTS * TILES, :], T["consts"][0:PARTS * TILES, C_SPREAD:C_WIDTH]
                            ).then_inc(s_small, 16)
                e.dma_start(src_i[:, :], T["src_c"]).then_inc(s_edge, 16)
                e.dma_start(dst_bc[:, 0, 0:GE], T["dst_row"][0:P, :]).then_inc(s_gd, 16)
                e.dma_start(dst_bc[0:NG - P, 1, 0:GE], T["dst_row"][P:NG, :]).then_inc(s_gd, 16)
                e.dma_start(X[:, :].rearrange("p (b f) -> p b f", f=F),
                            T["x"].rearrange("(b p) f -> p b f", p=P)).then_inc(s_edge, 16)
                e.dma_start(weight[:, :], T["weight_c"]).then_inc(s_edge, 16)
                e.dma_start(iota[:, :], T["iota"].to_broadcast([P, NP_])).then_inc(s_iota, 16)
                e.wait_ge(s_rng, 1)
                e.dma_start(range_dst[0:P, :], small[:, 4:6].bitcast(i32)).then_inc(s_rng_out, 16)
                e.dma_start(range_dst[P:NG, :], small[0:NG - P, 6:8].bitcast(i32)).then_inc(s_rng_out, 16)
                e.wait_ge(s_rng_out, 32)
                e.dma_start(table_dst[:, :], range_dst.rearrange("(a g) c -> a (g c)", a=1)).then_inc(s_rng_in, 16)
                e.wait_ge(s_rng_in, 16)
                e.wait_ge(s_iota, 16)

            @block.scalar
            def _(e):
                e.dma_start(dst_f[:, :].bitcast(i32), T["dst_c"]).then_inc(s_edge, 16)
                e.dma_start(type_f[:, :].bitcast(i32), T["type_c"]).then_inc(s_edge, 16)
                for n in names:
                    e.dma_start(W[n][:, 0:F], T[n]).then_inc(s_w, 16)
                    n_w[0] += 16
                e.dma_start(attn[:, :], T["attn"]).then_inc(s_w, 16)
                e.dma_start(b1_col[:, :], T["b1_col"]).then_inc(s_w, 16)
                e.dma_start(rel_row[:, :], T["rel_row"].to_broadcast([P, N_RELS])).then_inc(s_w, 16)
                n_w[0] += 48
                for n in bias_names:
                    e.dma_start(bias[n][:, :], T[n].to_broadcast([P, F])).then_inc(s_w, 16)
                    n_w[0] += 16
                e.wait_ge(s_w, n_w[0])

            @block.vector
            def _(e):
                e.memset(one_col[:, :], 1.0)
                e.memset(one_f[:, :], 1.0)
                e.wait_ge(s_small, 32)
                e.tensor_copy(ident_h[:, :], ident)
                e.tensor_copy(spread[:, :], onehot_t[0:PARTS * TILES, :])
                e.wait_ge(s_gd, 32)
                for c, rows_ in ((0, P), (1, NG - P)):
                    e.tensor_reduce(small[0:rows_, 2 * c:2 * c + 1], dst_bc[0:rows_, c, 0:GE], AX, ALU.min)
                    e.tensor_reduce(small[0:rows_, 2 * c + 1:2 * c + 2], dst_bc[0:rows_, c, 0:GE], AX, ALU.max)
                e.drain()
                for c, rows_ in ((0, P), (1, NG - P)):
                    e.tensor_scalar(small[0:rows_, 2 * c + 1:2 * c + 2], small[0:rows_, 2 * c + 1:2 * c + 2],
                                    float(P), None, ALU.add)
                e.drain()
                for c, rows_ in ((0, P), (1, NG - P)):
                    e.tensor_copy(small[0:rows_, 8 + 2 * c:10 + 2 * c].bitcast(i32), small[0:rows_, 2 * c:2 * c + 2])
                e.drain()
                for c, rows_ in ((0, P), (1, NG - P)):
                    ins = e.tensor_scalar(small[0:rows_, 4 + 2 * c:6 + 2 * c].bitcast(i32),
                                          small[0:rows_, 8 + 2 * c:10 + 2 * c].bitcast(i32), 7, None,
                                          ALU.arith_shift_right)
                ins.then_inc(s_rng, 1)
                e.wait_ge(s_edge, 80)
                e.tensor_copy(dst_f[:, :], dst_f[:, :].bitcast(i32))
                e.tensor_copy(type_f[:, :], type_f[:, :].bitcast(i32))
                e.tensor_scalar(pos_i[:, :], src_i[:, :], 7, None, ALU.arith_shift_right)
                e.drain()
                e.tensor_copy(src_block[:, :], pos_i[:, :])
                e.drain()

        def node_products(tag, parts, w_out, finish, store=None):
            s_t, s_tc, s_o, s_f = sem(tag + "_t"), sem(tag + "_tc"), sem(tag + "_o"), sem(tag + "_f")
            k = len(parts)

            def run(block):
                @block.tensor
                def _(e):
                    def transposes(b):
                        if b >= 2:
                            e.wait_ge(s_tc, b - 1)
                        for n, (get, _) in enumerate(parts):
                            ins = e.matmul(wide[:, 512 * (b % 2) + n * P:512 * (b % 2) + (n + 1) * P], lhsT=get(b), rhs=ident,
                                           start=True, stop=True)
                        ins.then_inc(s_t, 1)

                    transposes(0)
                    for b in range(NB):
                        if b + 1 < NB:
                            transposes(b + 1)
                        e.wait_ge(s_tc, b + 1)
                        if b >= 2:
                            e.wait_ge(s_f, b - 1)
                        for n, (_, w) in enumerate(parts):
                            ins = e.matmul(bank[2 + b % 2][:, 0:w_out], lhsT=tT[:, b % 2, n * P:(n + 1) * P],
                                           rhs=w[:, 0:w_out], start=(n == 0), stop=(n == k - 1))
                        ins.then_inc(s_o, 1)

                @block.scalar
                def _(e):
                    for b in range(NB):
                        e.wait_ge(s_t, b + 1)
                        if b >= 2:
                            e.wait_ge(s_o, b - 1)
                        e.copy(tT[:, b % 2, 0:k * P], wide[:, 512 * (b % 2):512 * (b % 2) + k * P]).then_inc(s_tc, 1)

                @block.vector
                def _(e):
                    for b in range(NB):
                        e.wait_ge(s_o, b + 1)
                        finish(e, b, bank[2 + b % 2])
                        e.drain().then_inc(s_f, 1)
                    if store:
                        store(e)
            return run

        def layernorm(tag, to):
            s_v, s_sd, s_y, s_st = sem(tag + "_v"), sem(tag + "_sd"), sem(tag + "_y"), sem(tag + "_st")
            with nc.Block() as block:
                @block.vector
                def _(e):
                    for b in range(NB):
                        e.bn_stats(stats[:, :], Xv[:, b, :])
                        e.drain()
                        e.bn_aggr(mv[:, b, :], stats[:, :])
                        e.drain()
                    e.tensor_scalar(rstd[:, :], mv[:, :, 1], EPS, None, ALU.add).then_inc(s_v, 1)
                    e.wait_ge(s_sd, 1)
                    e.reciprocal(rstd[:, :], rstd[:, :])
                    e.drain()
                    for b in range(NB):
                        e.tensor_scalar(Xv[:, b, :], Xv[:, b, :], mv[:, b, 0:1], rstd[:, b:b + 1],
                                        ALU.subtract, ALU.mult)
                    e.drain().then_inc(s_y, 1)

                @block.scalar
                def _(e):
                    e.wait_ge(s_v, 1)
                    e.activation(rstd[:, :], rstd[:, :], ACT.Sqrt).then_inc(s_sd, 1)

                @block.sync
                def _(e):
                    e.wait_ge(s_y, 1)
                    if to is not None:
                        store_nodes(e, to, Xv, s_st)

        def store_nodes(e, to, view, s_st):
            if to is out:
                full = N_NODES // P
                e.dma_start(out[0:full * P, :].rearrange("(b p) f -> p b f", p=P), view[:, 0:full, :]).then_inc(s_st, 16)
                e.dma_start(out[full * P:N_NODES, :], view[0:N_NODES - full * P, full, :]).then_inc(s_st, 16)
                e.wait_ge(s_st, 32)
            else:
                e.dma_start(to.rearrange("(b p) f -> p b f", p=P), view).then_inc(s_st, 16)
                e.wait_ge(s_st, 16)

        def range_registers(e, tag):
            return e.alloc_register(tag + "_first"), e.alloc_register(tag + "_end")

        def block_range(e, table, g, regs):
            e.load(list(regs), table[0:1, bass.ds(2 * g, 2)])
            return (e.snap(regs[0], min_val=0, max_val=NB - 1), e.snap(regs[1], min_val=1, max_val=NB))

        def same_range(e, regs):
            return (e.snap(regs[0], min_val=0, max_val=NB - 1), e.snap(regs[1], min_val=1, max_val=NB))

        def keep_range(e, regs, kept):
            for new, old in zip(regs, kept):
                e.reg_mov(old, new)

        def mark(e, s):
            e.matmul(bank[7][0:1, 0:1], lhsT=one_col[:, 0:1], rhs=one_col[:, 0:1], start=True, stop=True).then_inc(s, 1)

        def pe_sums(e, lo, hi, half_ready, half_done, group_rows, width, c):
            with e.Fori(lo, hi):
                e.reg_add(c, c, 1)
                for h in range(2):
                    e.wait_ge(half_ready[h], c)
                    for t in range(4 * h, 4 * h + 4):
                        ins = e.matmul(bank[2 + h][:, 0:width], lhsT=onehot[:, t, :], rhs=group_rows[:, t, 0:width],
                                       start=(t == 4 * h), stop=(t == 4 * h + 3))
                    ins.then_inc(half_done[h], 1)

        def half_onehot(e, h, b, ids):
            return e.tensor_tensor(onehot[:, 4 * h:4 * h + 4, :],
                                   iota[:, bass.ds(b * P, P)].unsqueeze(1).to_broadcast([P, 4, P]),
                                   ids.to_broadcast([P, 4, P]), ALU.is_equal)

        def add_half(e, h, b, width, scaled):
            to, new = A[:, bass.ds(b * width, width)], bank[2 + h][:, 0:width]
            if scaled and h == 0:
                e.scalar_tensor_tensor(out=to, in0=to, scalar=scale_now[:, 0:1], in1=new, op0=ALU.mult, op1=ALU.add)
            else:
                e.tensor_tensor(to, to, new, ALU.add)

        def dve_sums_begin(e, tag, half_done, width):
            e.memset(A[:, 0:NB * width], 0.0)
            for h in range(2):
                e.memset(bank[2 + h][:, :], 0.0)
            e.drain()
            for h in range(2):
                e.sem_inc(half_done[h], 1)
            last_b = e.alloc_register(tag + "_last_b")
            e.reg_mov(last_b, 0)
            return counter(e, tag + "_dve_pairs"), last_b

        def dve_sums(e, lo, hi, half_ready, half_done, ids_of, c, last_b, width, scale=None):
            with e.Fori(lo, hi) as b:
                e.reg_add(c, c, 1)
                before = e.snap(last_b)
                for h in range(2):
                    e.wait_ge(half_done[h], c)
                    e.sem_inc(note["dve"], 1)
                    add_half(e, h, before, width, scale is not None)
                    half_onehot(e, h, b, ids_of(h)).then_inc(half_ready[h], 1)
                    if h == 0:
                        e.drain()
                if scale is not None:
                    e.tensor_copy(scale_now[:, :], scale[:, bass.ds(b, 1)])
                e.reg_mov(last_b, b)
                e.drain()

        def dve_sums_end(e, half_done, c, last_b, width, scaled=False):
            before = e.snap(last_b)
            e.reg_add(c, c, 1)
            for h in range(2):
                e.wait_ge(half_done[h], c)
                e.sem_inc(note["dve"], 1)
                add_half(e, h, before, width, scaled)
                e.drain()

        def counter(e, name, first=0):
            c = e.alloc_register(name)
            e.reg_mov(c, first)
            return c

        def gathers(tag, table, width, s_free):
            s_idx = sem(tag + "_idx")
            s_rows = [sem(f"{tag}_rows{s}") for s in range(SLOTS)]

            def run(block):
                @block.gpsimd
                def _(e):
                    with e.Fori(0, TURNS) as i:
                        for s in range(SLOTS):
                            e.wait_ge(s_free[s], i + 1)
                            e.tensor_copy(idx[:, s, :], src_i[:, bass.ds(i * (SLOTS * TILES) + s * TILES, TILES)]
                                          ).then_inc(s_idx, 1)
                            e.wait_ge(s_idx, i * SLOTS + (s + 1))
                            e.sem_inc(note["pool"], 1)
                            for t in range(TILES):
                                e.indirect_dma_start(
                                    out=rows[:, s, t, 0:width], out_offset=None, in_=table,
                                    in_offset=bass.IndirectOffsetOnAxis(ap=idx[:, s, t:t + 1], axis=0),
                                ).then_inc(s_rows[s], 16)
            return run, s_rows

        def load_dst_bc(e, s_free_, s_in):
            with e.Fori(0, TURNS) as i:
                for s in range(SLOTS):
                    k = s % 2
                    e.wait_ge(s_free_[k], i * 2 + (s // 2 + 1))
                    e.dma_start(dst_bc[:, k, :], T["dst_row"][bass.ds(i * SLOTS + s, 1), :].to_broadcast([P, GE])
                                ).then_inc(s_in[k], 16)

        note = {n: nc.alloc_semaphore(name="note_" + n) for n in ("dve", "pe", "act", "pool")}

        s_wa, s_wc, s_zst = sem("l0_wa"), sem("l0_wc"), sem("l0_zst")
        W0 = W["L0_gnn_Wt"]
        with nc.Block() as block:
            @block.tensor
            def _(e):
                e.matmul(bank[7][:, 0:2], lhsT=W["L0_gnn_W"][:, :], rhs=attn[:, :], start=True, stop=True
                         ).then_inc(s_wa, 1)

            @block.vector
            def _(e):
                e.wait_ge(s_wa, 1)
                e.tensor_copy(W0[:, F:F + 2], bank[7][:, 0:2]).then_inc(s_wc, 1)
                e.wait_ge(s_wc, 1)
        s_dst_n = sb("s_dst_n", [P, NB])
        far_node = sb("far_node", [P, NB])
        s_dst_p = sb("s_dst_p", [P, NB, PARTS], bf16)

        def finish_z(e, b, ps):
            e.tensor_copy(Z[:, b, 0:F + 2], ps[:, 0:F + 2])
            e.tensor_copy(s_dst_n[:, b:b + 1], ps[:, S_DST:S_DST + 1])
            if b < N_RELS:
                e.tensor_scalar(mask[:, :], type_f[:, :], float(b), rel_row[:, b:b + 1], ALU.is_equal, ALU.mult)
                e.drain()
                if b:
                    e.tensor_tensor(rel[:, :], rel[:, :], mask[:, :], ALU.add)
                else:
                    e.tensor_copy(rel[:, :], mask[:, :])

        Z = A_(ZW)
        Z_parts = A[:, 0:NB * ZW].bitcast(bf16).rearrange("p (b f) -> p b f", f=2 * ZW)[:, :, S_PARTS:S_PARTS + PARTS]
        assert N_RELS <= NB
        run = node_products("l0z", [(lambda b: Xv[:, b, :], W0)], F + 2, finish_z)
        with nc.Block() as block:
            run(block)
        s_parts = sem("l0_parts")
        rest = sb("rest", [P, NB])
        with nc.Block() as block:
            @block.vector
            def _(e):
                e.tensor_copy(Z_parts[:, :, 0], Z[:, :, S_SRC])
                e.memset(Z_parts[:, :, 3], 0.0)
                e.drain()
                e.tensor_tensor(rest[:, :], Z[:, :, S_SRC], Z_parts[:, :, 0], ALU.subtract)
                e.drain()
                e.tensor_copy(Z_parts[:, :, 1], rest[:, :])
                e.drain()
                e.tensor_tensor(rest[:, :], rest[:, :], Z_parts[:, :, 1], ALU.subtract)
                e.drain()
                e.tensor_copy(Z_parts[:, :, 2], rest[:, :])
                e.drain().then_inc(s_parts, 1)
                e.tensor_copy(s_dst_p[:, :, 0], s_dst_n[:, :])
                e.tensor_scalar(far_node[:, :], node_id, -FAR, None, ALU.mult)
                e.drain()
                e.tensor_tensor(rest[:, :], s_dst_n[:, :], s_dst_p[:, :, 0], ALU.subtract)
                e.drain()
                e.tensor_copy(s_dst_p[:, :, 1], rest[:, :])
                e.drain()
                e.tensor_tensor(s_dst_p[:, :, 2], rest[:, :], s_dst_p[:, :, 1], ALU.subtract)
                e.drain()

            @block.sync
            def _(e):
                e.wait_ge(s_parts, 1)
                store_nodes(e, z_table, Z, s_zst)

        away = sb("away", [P, GE])
        onehot_th = onehot_t[:, 0:GE // 2].bitcast(bf16)
        hid = sb("hid", [P, GE])
        s_max = sb("s_max", [P, NB])
        m_node = sb("m_node", [P, NB])
        m_step = sb("m_step", [P, 2, NB])
        m_scale = sb("m_scale", [P, 2, NB])
        scale_now = sb("scale_now", [P, 1])
        q = sb("q", [P, 6], bf16)
        m_now = sb("m_now", [P, 3])
        look_sum = sb("look_sum", [P, TILES * 6])
        look_all = sb("look_all", [P, TILES, 2])
        e_edge = sb("e_edge", [P, TILES])
        num = sb("num", [P, TILES])
        row_scale = sb("row_scale", [P, TILES])
        s_src_p = sb("s_src_p", [P, PARTS * TILES], bf16)
        s_src_t = sb("s_src_t", [PARTS * TILES, P], bf16)
        rows_h = rows[:, :, :, :].rearrange("p s t w -> p (s t w)").bitcast(bf16).rearrange(
            "p (s t w) -> p s t w", s=SLOTS, t=TILES)
        s_free = [sem(f"l0_free{s}") for s in range(SLOTS)]
        run_gather, s_rows = gathers("l0g", z_table, ZW, s_free)
        s_bc = [sem(f"l0_bc{k}") for k in range(2)]
        s_bcf = [sem(f"l0_bcf{k}") for k in range(2)]
        s_ot, s_away, s_away_free, s_picked, s_turned, s_brought, s_sbc, s_q, s_look, s_ee, s_num, s_w_, s_scaled = (
            sem("l0_" + n) for n in ("ot", "away", "away_free", "picked", "turned", "brought", "sbc", "q", "look", "ee", "num", "w", "scaled"))
        half_ready, half_done = ([sem(f"l0_{n}{h}") for h in range(2)] for n in ("ready_half", "done_half"))
        look = bank[4][:, 0:6 * TILES]
        with nc.Block() as block:
            run_gather(block)

            @block.sync
            def _(e):
                load_dst_bc(e, s_bcf, s_bc)

            @block.scalar
            def _(e):
                def bring(g, i, s):
                    e.wait_ge(s_rows[s], (i + 1) * 16 * TILES)
                    e.sem_inc(note["act"], 1)
                    e.copy(s_src_p[:, :].rearrange("p (t k) -> p t k", k=PARTS),
                           rows_h[:, s, :, S_PARTS:S_PARTS + PARTS]).then_inc(s_picked, 1)
                    e.wait_ge(s_turned, g + 1)
                    e.sem_inc(note["act"], 1)
                    e.copy(s_src_t[:, :], bank[5][0:PARTS * TILES, 0:P]).then_inc(s_brought, 1)

                def scale_rows(g, s):
                    e.wait_ge(s_w_, g + 1)
                    e.sem_inc(note["act"], 1)
                    for t in range(TILES):
                        ins = e.activation(rows[:, s, t, 0:F], rows[:, s, t, 0:F], ACT.Copy,
                                           scale=row_scale[:, t:t + 1])
                    ins.then_inc(s_scaled, 1)

                c = counter(e, "l0_act_pairs", 1)
                regs = range_registers(e, "l0_act")
                before = e.alloc_register("l0_act_before")
                for k in range(2):
                    e.sem_inc(s_bcf[k], 1)
                e.reg_mov(before, 0)
                for first in (s_away, s_ot, s_q, s_look, s_away_free, s_away_free):
                    e.sem_inc(first, 1)
                bring(0, 0, 0)
                with e.Fori(0, TURNS) as i:
                    for s in range(SLOTS):
                        g, k = i * SLOTS + s, s % 2
                        lo, hi = block_range(e, table_dst, g, regs)
                        e.wait_ge(s_bc[k], (i * 2 + (s // 2 + 1)) * 16)
                        e.sem_inc(note["act"], 1)
                        with e.Fori(lo, hi) as b:
                            e.wait_ge(s_ot, c)
                            e.wait_ge(s_look, c)
                            e.reg_add(c, c, 1)
                            e.wait_ge(s_away_free, c)
                            e.sem_inc(note["act"], 1)
                            e.activation(away[:, :], dst_bc[:, k, :], ACT.Square, scale=FAR,
                                         bias=far_node[:, bass.ds(b, 1)]).then_inc(s_away, 1)
                            e.wait_ge(s_away, c)
                            e.sem_inc(note["act"], 1)
                            ins = e.activation(onehot_th, away[:, :], ACT.Relu, scale=-1.0, bias=one_f[:, 0:1])
                            ins.then_inc(s_ot, 1)
                        e.drain().then_inc(s_bcf[k], 1)
                        if s:
                            scale_rows(g - 1, s - 1)
                        else:
                            with e.If(i > 0):
                                scale_rows(e.snap(before, min_val=0, max_val=NG - 1), SLOTS - 1)
                        if s < SLOTS - 1:
                            bring(g + 1, i, s + 1)
                        else:
                            with e.If(i < TURNS - 1):
                                bring(g + 1, i + 1, 0)
                        e.wait_ge(s_ee, g + 1)
                        e.sem_inc(note["act"], 1)
                        e.activation(num[:, :], e_edge[:, :], ACT.Exp)
                        e.activation(m_scale[:, k, :], m_step[:, k, :], ACT.Exp).then_inc(s_num, 1)
                    e.reg_mov(before, i * SLOTS + (SLOTS - 1))
                scale_rows(NG - 1, SLOTS - 1)

            @block.tensor
            def _(e):
                c = counter(e, "l0_pe_looks", 1)
                c2 = counter(e, "l0_pe_pairs")
                regs = range_registers(e, "l0_pe")
                regs2 = range_registers(e, "l0_pe2")
                e.reg_mov(regs2[0], 0)
                e.reg_mov(regs2[1], 1)
                before = e.alloc_register("l0_pe2_before")
                e.reg_mov(before, 0)

                def spread_s(g):
                    e.wait_ge(s_picked, g + 1)
                    e.sem_inc(note["pe"], 1)
                    e.matmul(bank[5][0:PARTS * TILES, 0:P], lhsT=s_src_p[:, :],
                             rhs=ident_h[:, :], start=True, stop=True).then_inc(s_turned, 1)
                    e.wait_ge(s_brought, g + 1)
                    e.sem_inc(note["pe"], 1)
                    for t in range(TILES):
                        ins = e.matmul(wide[:, t * P:(t + 1) * P],
                                       lhsT=spread[:, t * P:(t + 1) * P], rhs=s_src_t[:, :], start=True, stop=True)
                    ins.then_inc(s_sbc, 1)

                def sums(g, s):
                    lo, hi = same_range(e, regs2)
                    e.wait_ge(s_scaled, g + 1)
                    e.sem_inc(note["pe"], 1)
                    pe_sums(e, lo, hi, half_ready, half_done, rows[:, s, :, :], MW, c2)
                    mark(e, s_free[s])

                for s in range(SLOTS):
                    e.sem_inc(s_free[s], 1)
                spread_s(0)
                with e.Fori(0, TURNS) as i:
                    for s in range(SLOTS):
                        g = i * SLOTS + s
                        lo, hi = block_range(e, table_dst, g, regs)
                        with e.Fori(lo, hi):
                            e.reg_add(c, c, 1)
                            e.wait_ge(s_ot, c)
                            e.wait_ge(s_q, c)
                            e.sem_inc(note["pe"], 1)
                            for t in range(TILES):
                                ins = e.matmul(look[:, 6 * t:6 * t + 6], lhsT=onehot_th[:, t * P:(t + 1) * P],
                                               rhs=q[:, :], start=True, stop=True)
                            ins.then_inc(s_look, 1)
                        if s < SLOTS - 1:
                            spread_s(g + 1)
                        else:
                            with e.If(i < TURNS - 1):
                                spread_s(g + 1)
                        if s:
                            sums(g - 1, s - 1)
                        else:
                            with e.If(i > 0):
                                sums(e.snap(before, min_val=0, max_val=NG - 1), SLOTS - 1)
                        keep_range(e, regs, regs2)
                    e.reg_mov(before, i * SLOTS + (SLOTS - 1))
                sums(NG - 1, SLOTS - 1)

            @block.vector
            def _(e):
                e.memset(s_max[:, :], -HUGE)
                e.memset(m_node[:, :], -HUGE * SLOPE)
                e.memset(m_step[:, :, :], 0.0)
                e.memset(scale_now[:, :], 1.0)
                c2, last_b = dve_sums_begin(e, "l0", half_done, MW)
                c = counter(e, "l0_dve_looks", 1)
                regs = range_registers(e, "l0_dve")
                regs2 = range_registers(e, "l0_dve2")
                e.reg_mov(regs2[0], 0)
                e.reg_mov(regs2[1], 1)
                before = e.alloc_register("l0_dve2_before")
                e.reg_mov(before, 0)
                def sums(g, k):
                    lo, hi = same_range(e, regs2)
                    dve_sums(e, lo, hi, half_ready, half_done,
                             lambda h: dst_f[:, bass.ds(g * TILES + 4 * h, 4)].unsqueeze(2), c2, last_b, MW,
                             m_scale[:, k, :])

                with e.Fori(0, TURNS) as i:
                    for s in range(SLOTS):
                        g, k = i * SLOTS + s, s % 2
                        lo, hi = block_range(e, table_dst, g, regs)
                        e.memset(look_sum[:, :], 0.0)
                        with e.Fori(lo, hi) as b:
                            e.reg_add(c, c, 1)
                            e.tensor_copy(small[:, 16:17], s_max[:, bass.ds(b, 1)])
                            e.tensor_copy(m_now[:, 1:2], s_dst_n[:, bass.ds(b, 1)])
                            e.tensor_copy(q[:, 0:3], s_dst_p[:, bass.ds(b, 1), 0:3].rearrange("p a k -> p (a k)"))
                            e.drain()
                            e.wait_ge(s_away, c)
                            e.wait_ge(s_sbc, g + 1)
                            e.sem_inc(note["dve"], 1)
                            e.tensor_tensor_reduce(out=hid[:, :], in0=wide[:, :], in1=away[:, :], scale=1.0,
                                                   scalar=small[:, 16:17], op0=ALU.subtract, op1=ALU.max,
                                                   accum_out=small[:, 17:18])
                            e.drain().then_inc(s_away_free, 1)
                            e.tensor_tensor(small[:, 19:20], small[:, 17:18], m_now[:, 1:2], ALU.add)
                            e.drain()
                            for m_to in (m_now[:, 0:1], q[:, 3:4]):
                                e.scalar_tensor_tensor(out=m_to, in0=small[:, 19:20], scalar=SLOPE,
                                                       in1=small[:, 19:20], op0=ALU.mult, op1=ALU.max)
                            e.drain()
                            for m_rest in (m_now[:, 1:2], q[:, 4:5]):
                                e.tensor_tensor(m_rest, m_now[:, 0:1], q[:, 3:4], ALU.subtract)
                            e.drain()
                            e.tensor_tensor(q[:, 5:6], m_now[:, 1:2], q[:, 4:5], ALU.subtract).then_inc(s_q, 1)
                            e.tensor_copy(s_max[:, bass.ds(b, 1)], small[:, 17:18])
                            e.tensor_tensor(m_step[:, k, bass.ds(b, 1)], m_node[:, bass.ds(b, 1)], m_now[:, 0:1],
                                            ALU.subtract)
                            e.drain()
                            e.tensor_copy(m_node[:, bass.ds(b, 1)], m_now[:, 0:1])
                            e.wait_ge(s_look, c)
                            e.sem_inc(note["dve"], 1)
                            e.tensor_tensor(look_sum[:, :], look_sum[:, :], look, ALU.add)
                            e.drain()
                        e.tensor_reduce(look_all[:, :, :].rearrange("p t c -> p (t c)"),
                                        look_sum[:, :].rearrange("p (n k) -> p n k", k=3), AX, ALU.add)
                        e.drain()
                        e.tensor_tensor(e_edge[:, :], rows[:, s, :, S_SRC], look_all[:, :, 0], ALU.add)
                        e.drain()
                        e.scalar_tensor_tensor(out=e_edge[:, :], in0=e_edge[:, :], scalar=SLOPE, in1=e_edge[:, :],
                                               op0=ALU.mult, op1=ALU.max)
                        e.drain()
                        e.tensor_tensor(e_edge[:, :], e_edge[:, :], look_all[:, :, 1], ALU.subtract).then_inc(s_ee, 1)
                        if s:
                            sums(g - 1, 1 - k)
                        else:
                            with e.If(i > 0):
                                sums(e.snap(before, min_val=0, max_val=NG - 1), 1 - k)
                        keep_range(e, regs, regs2)
                        e.wait_ge(s_num, g + 1)
                        e.sem_inc(note["dve"], 1)
                        e.tensor_copy(rows[:, s, :, F], num[:, :])
                        e.tensor_tensor(row_scale[:, :], num[:, :], rel[:, bass.ds(g * TILES, TILES)], ALU.mult
                                        ).then_inc(s_w_, 1)
                    e.reg_mov(before, i * SLOTS + (SLOTS - 1))
                sums(NG - 1, (NG - 1) % 2)
                dve_sums_end(e, half_done, c2, last_b, MW, True)

        rden = sb("rden", [P, NB])
        A0 = A_(MW)
        with nc.Block() as block:
            @block.vector
            def _(e):
                e.tensor_scalar(rden[:, :], A0[:, :, F], TINY, None, ALU.max)
                e.drain()
                e.reciprocal(rden[:, :], rden[:, :])
                e.drain()
                for b in range(NB):
                    e.scalar_tensor_tensor(out=Xv[:, b, :], in0=A0[:, b, 0:F], scalar=rden[:, b:b + 1],
                                           in1=Xv[:, b, :], op0=ALU.mult, op1=ALU.add)
                e.drain()
                e.tensor_tensor(Xv, Xv, bias["L0_gnn_bias_w"][:, :].unsqueeze(1).to_broadcast([P, NB, F]), ALU.add)
                e.memset(rows[:, :, :, F], 1.0)
                e.drain()
        layernorm("l0n", x_tables[0])
        release_semaphores()

        def sum_pass(tag, table, weighted, extra):
            width = F if weighted else MW
            s_free = [sem(f"{tag}_free{s}") for s in range(SLOTS)]
            run_gather, s_rows = gathers(tag, table, F, s_free)
            s_ready = [sem(f"{tag}_ready{s}") for s in range(SLOTS)]
            half_ready, half_done = ([sem(f"{tag}_{n}{h}") for h in range(2)] for n in ("ready_half", "done_half"))
            with nc.Block() as block:
                run_gather(block)
                if weighted:
                    @block.scalar
                    def _(e):
                        with e.Fori(0, TURNS) as i:
                            for s in range(SLOTS):
                                e.wait_ge(s_rows[s], (i + 1) * 16 * TILES)
                                e.sem_inc(note["act"], 1)
                                for t in range(TILES):
                                    ins = e.activation(
                                        rows[:, s, t, 0:F], rows[:, s, t, 0:F], ACT.Copy,
                                        scale=weight[:, bass.ds(i * (SLOTS * TILES) + (s * TILES + t), 1)])
                                ins.then_inc(s_ready[s], 1)

                @block.tensor
                def _(e):
                    c = counter(e, tag + "_pe_pairs")
                    regs = range_registers(e, tag + "_pe")
                    for s in range(SLOTS):
                        e.sem_inc(s_free[s], 1)
                    with e.Fori(0, TURNS) as i:
                        for s in range(SLOTS):
                            lo, hi = block_range(e, table_dst, i * SLOTS + s, regs)
                            if weighted:
                                e.wait_ge(s_ready[s], i + 1)
                            else:
                                e.wait_ge(s_rows[s], (i + 1) * 16 * TILES)
                            e.sem_inc(note["pe"], 1)
                            pe_sums(e, lo, hi, half_ready, half_done, rows[:, s, :, :], width, c)
                            mark(e, s_free[s])

                @block.vector
                def _(e):
                    c, last_b = dve_sums_begin(e, tag, half_done, width)
                    regs = range_registers(e, tag + "_dve")
                    with e.Fori(0, TURNS) as i:
                        if extra:
                            extra(e, i)
                        for s in range(SLOTS):
                            g = i * SLOTS + s
                            lo, hi = block_range(e, table_dst, g, regs)
                            dve_sums(e, lo, hi, half_ready, half_done,
                                     lambda h: dst_f[:, bass.ds(g * TILES + 4 * h, 4)].unsqueeze(2), c, last_b, width)
                    dve_sums_end(e, half_done, c, last_b, width)

        def count_bucket(e, i):
            e.tensor_scalar(mask[:, :], src_block[:, :], iota[:, bass.ds(i, 1)], None, ALU.is_equal)
            e.drain()
            e.tensor_reduce(tot[:, bass.ds(i, 1)], mask[:, :], AX, ALU.add)

        def place_bucket(e, i):
            e.tensor_scalar(mask[:, :], src_block[:, :], iota[:, bass.ds(i, 1)], None, ALU.is_equal)
            e.tensor_copy(small[:, 20:21], base[:, bass.ds(i, 1)])
            e.drain()
            e.tensor_tensor_scan(cum[:, :], mask[:, :], mask[:, :], small[:, 20:21], ALU.add, ALU.max)
            e.drain()
            e.copy_predicated(pos[:, :], mask[:, :].bitcast(u32), cum[:, :])
            e.drain()

        sum_pass("l1", x_tables[0], False, count_bucket)

        s_tot, s_ps, s_base, s_ro, s_ri = sem("so_tot"), sem("so_ps"), sem("so_base"), sem("so_ro"), sem("so_ri")
        with nc.Block() as block:
            @block.tensor
            def _(e):
                e.matmul(bank[4][:, 0:NB], lhsT=tri, rhs=tot[:, :], start=True, stop=True)
                e.matmul(bank[5][:, 0:NB], lhsT=ones, rhs=tot[:, :], start=True, stop=True).then_inc(s_ps, 1)

            @block.vector
            def _(e):
                e.wait_ge(s_ps, 1)
                e.tensor_copy(tot[:, :], bank[5][:, 0:NB])
                e.drain()
                e.tensor_tensor_scan(end_of[:, :], tot[:, :], tot[:, :], 0.0, ALU.add, ALU.max)
                e.drain()
                e.tensor_tensor(start_of[:, :], end_of[:, :], bank[5][:, 0:NB], ALU.subtract)
                e.drain()
                e.tensor_tensor(base[:, :], start_of[:, :], bank[4][:, 0:NB], ALU.add)
                for c in range(2):
                    e.tensor_scalar(cum[:, 0:NB], end_of[:, :], group_at[:, c:c + 1], None, ALU.is_le)
                    e.tensor_scalar(mask[:, 0:NB], start_of[:, :], group_at[:, c:c + 1], float(GE - 1),
                                    ALU.subtract, ALU.is_le)
                    e.drain()
                    e.tensor_reduce(small[:, 24 + 2 * c:25 + 2 * c], cum[:, 0:NB], AX, ALU.add)
                    e.tensor_reduce(small[:, 25 + 2 * c:26 + 2 * c], mask[:, 0:NB], AX, ALU.add)
                    e.drain()
                    ins = e.tensor_copy(small[:, 28 + 2 * c:30 + 2 * c].bitcast(i32), small[:, 24 + 2 * c:26 + 2 * c])
                    e.drain()
                e.drain().then_inc(s_base, 1)

            @block.sync
            def _(e):
                e.wait_ge(s_base, 1)
                for c in range(2):
                    e.dma_start(range_src[c * HG:(c + 1) * HG, :], small[0:HG, 28 + 2 * c:30 + 2 * c].bitcast(i32)
                                ).then_inc(s_ro, 16)
                e.wait_ge(s_ro, 32)
                e.dma_start(table_src[:, :], range_src.rearrange("(a g) c -> a (g c)", a=1)).then_inc(s_ri, 16)
                e.wait_ge(s_ri, 16)

        A1 = A_(MW)
        with nc.Block() as block:
            @block.vector
            def _(e):
                e.tensor_scalar(rden[:, :], A1[:, :, F], 1.0, None, ALU.max)
                e.drain()
                e.reciprocal(rden[:, :], rden[:, :])
                e.drain()
                for b in range(NB):
                    e.tensor_scalar(A1[:, b, 0:F], A1[:, b, 0:F], rden[:, b:b + 1], None, ALU.mult)
                e.drain()

        def add_to_x(e, b, ps):
            e.tensor_tensor(Xv[:, b, :], Xv[:, b, :], ps[:, 0:F], ALU.add)

        run = node_products("l1d", [(lambda b: A1[:, b, 0:F], W["L1_gnn_W_lt"]), (lambda b: Xv[:, b, :], W["L1_gnn_W_rt"])],
                            F, add_to_x)
        with nc.Block() as block:
            run(block)
        layernorm("l1n", x_tables[1])
        release_semaphores()

        A2 = A_(F)
        Hv = H[:, :].rearrange("p (b f) -> p b f", f=F)
        for k in range(3):
            sum_pass(f"l2{k}", x_tables[1 + k] if k < 2 else x_tables[3], True, place_bucket if k == 0 else None)
            b_row = bias[f"L2_gnn_b_rel{k + 1}"]

            def finish_conv(e, b, ps, k=k, b_row=b_row):
                if k < 2:
                    e.tensor_tensor(Hv[:, b, :], ps[:, 0:F], b_row[:, :], ALU.add)
                    e.drain()
                    e.tensor_scalar(Hv[:, b, :], Hv[:, b, :], 0.0, None, ALU.max)
                else:
                    e.tensor_tensor(Xv[:, b, :], Xv[:, b, :], ps[:, 0:F], ALU.add)
                    e.drain()
                    e.tensor_tensor(Xv[:, b, :], Xv[:, b, :], b_row[:, :], ALU.add)

            own = Xv if k == 0 else Hv
            run = node_products(f"l2d{k}", [(lambda b: A2[:, b, :], W[f"L2_gnn_W_rel{k + 1}t"]),
                                            (lambda b, own=own: own[:, b, :], W[f"L2_gnn_W_root{k + 1}t"])],
                                F, finish_conv)
            with nc.Block() as block:
                run(block)
            if k < 2:
                s_hst = sem(f"l2_hst{k}")
                with nc.Block() as block:
                    @block.sync
                    def _(e):
                        store_nodes(e, x_tables[2 + k], Hv, s_hst)
        layernorm("l2n", None)
        release_semaphores()

        def finish_h(e, b, ps):
            e.tensor_tensor(Hv[:, b, :], ps[:, 0:F], bias["L3_gnn_bl"][:, :], ALU.add)

        s_pos = sem("s_pos")
        run = node_products("l3h", [(lambda b: Xv[:, b, :], W["L3_gnn_Wl"])], F, finish_h)
        with nc.Block() as block:
            run(block)

            @block.gpsimd
            def _(e):
                e.tensor_scalar(pos[:, :], pos[:, :], -1.0, None, ALU.add).then_inc(s_pos, 1)
                e.wait_ge(s_pos, 1)
                e.tensor_copy(pos_i[:, :], pos[:, :]).then_inc(s_pos, 1)
                e.wait_ge(s_pos, 2)

        attr = onehot[:, :, :].rearrange("p (k t) n -> p k (t n)", k=2)
        h_edge = away
        s_bc = [sem(f"l3_bc{k}") for k in range(2)]
        s_bcf = [sem(f"l3_bcf{k}") for k in range(2)]
        s_at = [sem(f"l3_at{k}") for k in range(2)]
        s_atf = [sem(f"l3_atf{k}") for k in range(2)]
        s_msg, s_mm1, s_hid, s_mm2, s_wf, s_ot, s_g, s_idx, s_nt = (
            sem("l3_" + n) for n in ("msg", "mm1", "hid", "mm2", "wf", "ot", "g", "idx", "nt"))
        s_scat = [sem(f"l3_scat{s}") for s in range(SLOTS)]
        with nc.Block() as block:
            @block.sync
            def _(e):
                with e.Fori(0, TURNS) as i:
                    for s in range(SLOTS):
                        k = s % 2
                        e.wait_ge(s_bcf[k], i * 2 + (s // 2 + 1))
                        e.dma_start(dst_bc[:, k, :], T["dst_row"][bass.ds(i * SLOTS + s, 1), :].to_broadcast([P, GE])
                                    ).then_inc(s_bc[k], 16)
                        e.wait_ge(s_atf[k], i * 2 + (s // 2 + 1))
                        e.dma_start(attr[:, k, :], T["attr_t"][bass.ds(i * SLOTS + s, 1), :, :].rearrange(
                            "a p n -> (a p) n")).then_inc(s_at[k], 16)

            @block.tensor
            def _(e):
                c = counter(e, "l3_pe_pairs")
                regs = range_registers(e, "l3_pe")
                for k in range(2):
                    e.sem_inc(s_atf[k], 1)
                with e.Fori(0, TURNS) as i:
                    for s in range(SLOTS):
                        g, k = i * SLOTS + s, s % 2
                        lo, hi = block_range(e, table_dst, g, regs)
                        e.wait_ge(s_at[k], (i * 2 + (s // 2 + 1)) * 16)
                        e.sem_inc(s_nt, 1)
                        for h in range(2):
                            r = slice(h * N_RBF, (h + 1) * N_RBF)
                            ins = e.matmul(wide[:, h * 512:(h + 1) * 512], lhsT=W["L3_gnn_W1d"][r, 0:F], rhs=attr[r, k, :],
                                           start=True, stop=True)
                        ins.then_inc(s_mm1, 1)
                        e.wait_ge(s_hid, g + 1)
                        e.sem_inc(s_nt, 1)
                        e.drain().then_inc(s_atf[k], 1)
                        e.wait_ge(s_wf, g + 1)
                        e.sem_inc(s_nt, 1)
                        for t in range(TILES):
                            ins = e.matmul(bank[2 + t // 4][:, (t % 4) * P:(t % 4 + 1) * P],
                                           lhsT=hid[:, t * P:(t + 1) * P], rhs=W["L3_gnn_W2"][:, :],
                                           start=True, stop=True)
                        ins.then_inc(s_mm2, 1)
                        with e.Fori(lo, hi) as b:
                            e.reg_add(c, c, 1)
                            e.wait_ge(s_ot, c)
                            e.sem_inc(s_nt, 1)
                            for t in range(TILES):
                                ins = e.matmul(bank[4 + t // 4][:, (t % 4) * P:(t % 4 + 1) * P],
                                               lhsT=onehot_t[:, t * P:(t + 1) * P], rhs=H[:, bass.ds(b * F, F)],
                                               start=True, stop=True)
                            ins.then_inc(s_g, 1)

            @block.scalar
            def _(e):
                with e.Fori(0, NG) as g:
                    e.wait_ge(s_mm1, g + 1)
                    for h in range(2):
                        ins = e.activation(hid[:, h * 512:(h + 1) * 512], wide[:, h * 512:(h + 1) * 512], ACT.Relu, bias=b1_col[:, 0:1])
                    ins.then_inc(s_hid, 1)

            @block.vector
            def _(e):
                c = counter(e, "l3_dve_pairs")
                regs = range_registers(e, "l3_dve")
                for k in range(2):
                    e.sem_inc(s_bcf[k], 1)
                e.sem_inc(s_wf, 1)
                with e.Fori(0, TURNS) as i:
                    for s in range(SLOTS):
                        g, k = i * SLOTS + s, s % 2
                        lo, hi = block_range(e, table_dst, g, regs)
                        e.memset(h_edge[:, :], 0.0)
                        e.wait_ge(s_bc[k], (i * 2 + (s // 2 + 1)) * 16)
                        e.sem_inc(s_nt, 1)
                        with e.Fori(lo, hi) as b:
                            e.reg_add(c, c, 1)
                            e.tensor_scalar(onehot_t[:, :], dst_bc[:, k, :], node_id[:, bass.ds(b, 1)], None, ALU.is_equal)
                            e.drain().then_inc(s_ot, 1)
                            e.wait_ge(s_g, c)
                            for h in range(2):
                                r = slice(h * 512, (h + 1) * 512)
                                e.tensor_tensor(h_edge[:, r], h_edge[:, r], bank[4 + h][:, :], ALU.add)
                            e.drain()
                        e.drain().then_inc(s_bcf[k], 1)
                        with e.If(i > 0):
                            e.wait_ge(s_scat[s], i * (16 * TILES))
                            e.sem_inc(s_nt, 1)
                        e.wait_ge(s_mm2, g + 1)
                        for h in range(2):
                            e.tensor_tensor(rows[:, s, 4 * h:4 * h + 4, 0:F],
                                            bank[2 + h][:, :].rearrange("p (t f) -> p t f", f=F),
                                            bias["L3_gnn_b2"][:, :].unsqueeze(1).to_broadcast([P, 4, F]), ALU.add)
                        e.tensor_copy(rows[:, s, :, F], src_i[:, bass.ds(g * TILES, TILES)])
                        e.drain().then_inc(s_wf, 1)
                        e.tensor_tensor(rows[:, s, :, 0:F], rows[:, s, :, 0:F],
                                        h_edge[:, :].rearrange("p (t f) -> p t f", f=F), ALU.mult)
                        e.drain().then_inc(s_msg, 1)

            @block.gpsimd
            def _(e):
                with e.Fori(0, TURNS) as i:
                    for s in range(SLOTS):
                        e.wait_ge(s_msg, i * SLOTS + (s + 1))
                        e.tensor_copy(idx[:, s, :], pos_i[:, bass.ds(i * (SLOTS * TILES) + s * TILES, TILES)]
                                      ).then_inc(s_idx, 1)
                        e.wait_ge(s_idx, i * SLOTS + (s + 1))
                        e.sem_inc(s_nt, 1)
                        for t in range(TILES):
                            e.indirect_dma_start(
                                out=sorted_rows, out_offset=bass.IndirectOffsetOnAxis(ap=idx[:, s, t:t + 1], axis=0),
                                in_=rows[:, s, t, 0:MW], in_offset=None).then_inc(s_scat[s], 16)
                for s in range(SLOTS):
                    e.wait_ge(s_scat[s], TURNS * 16 * TILES)

        s_in = [sem(f"l3_in{s}") for s in range(SLOTS)]
        s_inf = [sem(f"l3_inf{s}") for s in range(SLOTS)]
        half_ready, half_done = ([sem(f"l3b_{n}{h}") for h in range(2)] for n in ("ready_half", "done_half"))
        msgs = [rows[:, s, :, :].rearrange("p t w -> p (t w)")[:, 0:TILES * MW] for s in range(SLOTS)]
        sorted_v = sorted_rows.rearrange("(g p t) w -> g p (t w)", p=P, t=TILES)
        with nc.Block() as block:
            @block.sync
            def _(e):
                with e.Fori(0, TURNS) as i:
                    for s in range(SLOTS):
                        e.wait_ge(s_inf[s], i + 1)
                        e.dma_start(msgs[s], sorted_v[bass.ds(i * SLOTS + s, 1), :, :].rearrange("a p n -> (a p) n")
                                    ).then_inc(s_in[s], 16)

            @block.tensor
            def _(e):
                c = counter(e, "l3b_pe_pairs")
                regs = range_registers(e, "l3b_pe")
                for s in range(SLOTS):
                    e.sem_inc(s_inf[s], 1)
                with e.Fori(0, TURNS) as i:
                    for s in range(SLOTS):
                        lo, hi = block_range(e, table_src, i * SLOTS + s, regs)
                        e.wait_ge(s_in[s], (i + 1) * 16)
                        e.sem_inc(note["pe"], 1)
                        pe_sums(e, lo, hi, half_ready, half_done, msgs[s].rearrange("p (t w) -> p t w", w=MW), F, c)
                        mark(e, s_inf[s])

            @block.vector
            def _(e):
                c, last_b = dve_sums_begin(e, "l3b", half_done, F)
                regs = range_registers(e, "l3b_dve")
                with e.Fori(0, TURNS) as i:
                    for s in range(SLOTS):
                        lo, hi = block_range(e, table_src, i * SLOTS + s, regs)
                        e.wait_ge(s_in[s], (i + 1) * 16)
                        e.sem_inc(note["dve"], 1)
                        mv_ = msgs[s].rearrange("p (t w) -> p t w", w=MW)
                        dve_sums(e, lo, hi, half_ready, half_done, lambda h: mv_[:, 4 * h:4 * h + 4, F:F + 1], c, last_b, F)
                dve_sums_end(e, half_done, c, last_b, F)
                e.tensor_tensor(X[:, :], X[:, :], A[:, 0:NB * F], ALU.add)
                e.drain()
        layernorm("l3n", out)


def kernel(**inputs):
    import numpy as np
    from concourse import bacc
    from concourse.bass_utils import run_bass_kernel_spmd

    a = {n: np.ascontiguousarray(np.asarray(v)) for n, v in inputs.items()}

    def padded(v, n, fill):
        o = np.full((n,) + v.shape[1:], fill, v.dtype)
        o[:v.shape[0]] = v
        return o

    def columns(v):
        return np.ascontiguousarray(v.reshape(NG, P, TILES).transpose(1, 0, 2).reshape(P, NG * TILES))

    dst = padded(a["dst"], EP, PAD_NODE)
    attr = padded(a["edge_attr_64"], EP, 0).reshape(NG, P, TILES, N_RBF)
    attr_t = np.ascontiguousarray(attr.transpose(0, 2, 3, 1).reshape(NG, 2, TILES // 2, N_RBF, P)
                                  .transpose(0, 1, 3, 2, 4).reshape(NG, 2 * N_RBF, GE // 2))
    consts = np.zeros((P, C_WIDTH), np.float32)
    consts[:, C_IDENT:C_IDENT + P] = np.eye(P)
    consts[:, C_TRI:C_TRI + P] = np.triu(np.ones((P, P)), 1)
    consts[:, C_ONES:C_ONES + P] = 1.0
    consts[:, C_NODE:C_NODE + NB] = np.arange(P)[:, None] + P * np.arange(NB)[None, :]
    consts[:, C_GROUP:C_GROUP + 2] = GE * (np.arange(P)[:, None] + HG * np.arange(2)[None, :])
    for k in range(PARTS * TILES):
        if k % PARTS < 3:
            t = k // PARTS
            consts[k, C_SPREAD + t * P:C_SPREAD + (t + 1) * P] = 1.0
    feeds = {
        "x": padded(a["x"], NP_, 0),
        "src_c": columns(padded(a["src"], EP, PAD_NODE)),
        "dst_c": columns(dst),
        "type_c": columns(padded(a["edge_type_40"], EP, 0)),
        "weight_c": columns(padded(a["edge_weight"], EP, 0)),
        "dst_row": np.ascontiguousarray(dst.reshape(NG, P, TILES).transpose(0, 2, 1).reshape(NG, GE)),
        "attr_t": attr_t,
        "consts": consts,
        "iota": np.arange(NP_, dtype=np.float32)[None, :],
        "L0_gnn_W": a["L0_gnn_W"],
        "L0_gnn_Wt": np.ascontiguousarray(a["L0_gnn_W"].T),
        "attn": np.ascontiguousarray(a["L0_gnn_attn_w"].reshape(2, F).T),
        "rel_row": a["L0_gnn_rel_emb"].reshape(1, N_RELS),
        "b1_col": a["L3_gnn_b1"].reshape(P, 1),
        "L3_gnn_W1d": np.concatenate([a["L3_gnn_W1"]] * 2, axis=0),
        "L3_gnn_W2": a["L3_gnn_W2"],
        "L3_gnn_Wl": a["L3_gnn_Wl"],
    }
    for n in ("L1_gnn_W_l", "L1_gnn_W_r", "L2_gnn_W_rel1", "L2_gnn_W_root1", "L2_gnn_W_rel2", "L2_gnn_W_root2",
              "L2_gnn_W_rel3", "L2_gnn_W_root3"):
        feeds[n + "t"] = np.ascontiguousarray(a[n].T)
    for n in ("L0_gnn_bias_w", "L2_gnn_b_rel1", "L2_gnn_b_rel2", "L2_gnn_b_rel3", "L3_gnn_b2", "L3_gnn_bl"):
        feeds[n] = a[n].reshape(1, F)

    nc = bacc.Bacc("TRN2", target_bir_lowering=False, num_devices=1)
    T = {n: nc.dram_tensor("in_" + n, v.shape, mybir.dt.from_np(v.dtype), kind="ExternalInput").ap()
         for n, v in feeds.items()}
    out = nc.dram_tensor("out_0", (N_NODES, F), f32, kind="ExternalOutput").ap()
    build_program(nc, T, out)
    r = run_bass_kernel_spmd(nc, [{"in_" + n: v for n, v in feeds.items()}], core_ids=[0])
    return r.results[0]["out_0"]
```

```python
from contextlib import ExitStack

import concourse.bass as bass
import concourse.mybir as mybir
from concourse.alu_op_type import AluOpType as ALU

P = 128
F = 128
N_NODES = 6250
N_EDGES = 200000
N_RELS = 40
N_RBF = 64
NB = -(-N_NODES // P)
NP_ = NB * P
TILES = 8
GE = TILES * P
NG = -(-N_EDGES // GE)
EP = NG * GE
SLOTS = 4
TURNS = NG // SLOTS
PAD_NODE = NP_ - 1
assert NG % SLOTS == 0 and TURNS == NB and PAD_NODE >= N_NODES
HG = NG // 2
ZW = F + 4
S_SRC, S_DST, S_PARTS = F, F + 1, 2 * (F + 2)
PARTS = 4
EARLY_RELS = 7
POOL_RELS = 9
MW = F + 1
HUGE = 3.0e38
TINY = 1.0e-30
EPS = 1.0e-5
SLOPE = 0.01
C_IDENT, C_TRI, C_ONES, C_NODE, C_GROUP = 0, P, 2 * P, 3 * P, 3 * P + NB
C_SPREAD = C_GROUP + 2
C_WIDTH = C_SPREAD + GE
FAR = 2.0 ** 51

f32 = mybir.dt.float32
bf16 = mybir.dt.bfloat16
i32 = mybir.dt.int32
u32 = mybir.dt.uint32
AX = mybir.AxisListType.X
ACT = mybir.ActivationFunctionType


def build_program(nc, T, out):
    ctx = ExitStack()
    with ctx:
        def sb(name, shape, dt=f32):
            return ctx.enter_context(nc.sbuf_tensor(name, shape, dt))

        live = []

        def sem(name):
            live.append(nc.alloc_semaphore(name=name))
            return live[-1]

        def release_semaphores():
            with nc.Block() as block:
                @block.gpsimd
                def _(e):
                    nc.clear_and_free_semaphores(list(live))
                    e.drain()
            live.clear()

        def dram(name, shape, dt=f32):
            return nc.dram_tensor(name, shape, dt, kind="Internal").ap()

        consts = sb("consts", [P, C_SPREAD])
        ident = consts[:, C_IDENT:C_IDENT + P]
        tri = consts[:, C_TRI:C_TRI + P]
        ones = consts[:, C_ONES:C_ONES + P]
        node_id = consts[:, C_NODE:C_NODE + NB]
        group_at = consts[:, C_GROUP:C_GROUP + 2]
        spread = sb("spread", [PARTS * TILES, GE], bf16)
        ident_h = sb("ident_h", [P, P], bf16)
        iota = sb("iota", [P, NP_])
        names = ["L0_gnn_W", "L0_gnn_Wt", "L1_gnn_W_lt", "L1_gnn_W_rt", "L2_gnn_W_rel1t", "L2_gnn_W_root1t",
                 "L2_gnn_W_rel2t", "L2_gnn_W_root2t", "L2_gnn_W_rel3t", "L2_gnn_W_root3t",
                 "L3_gnn_W1d", "L3_gnn_W2", "L3_gnn_Wl"]
        W = {n: sb("w_" + n, [P, F + 2 if n == "L0_gnn_Wt" else F]) for n in names}
        attn = sb("attn", [P, 2])
        bias_names = ["L0_gnn_bias_w", "L2_gnn_b_rel1", "L2_gnn_b_rel2", "L2_gnn_b_rel3", "L3_gnn_b2", "L3_gnn_bl"]
        bias = {n: sb("b_" + n, [P, F]) for n in bias_names}
        b1_col = sb("b1_col", [P, 1])
        rel_row = sb("rel_row", [P, N_RELS])
        src_i = sb("src_i", [P, NG * TILES], i32)
        dst_weight = sb("dst_weight", [P, 2 * NG * TILES])
        dst_f, weight = dst_weight[:, 0:NG * TILES], dst_weight[:, NG * TILES:2 * NG * TILES]
        type_f = sb("type_f", [P, NG * TILES])
        pos = type_f
        pos_i = sb("pos_i", [P, NG * TILES], i32)
        X = sb("X", [P, NB * F])
        A = sb("A", [P, NB * ZW])
        H = sb("H", [P, NB * F])
        src_block, mask, cum, rel = (H[:, k * NG * TILES:(k + 1) * NG * TILES] for k in range(4))
        rows = sb("rows", [P, SLOTS, TILES, ZW])
        idx = sb("idx", [P, SLOTS, TILES], i32)
        onehot = sb("onehot", [P, TILES, P])
        onehot_t = sb("onehot_t", [P, GE])
        dst_bc = sb("dst_bc", [P, 2, GE], i32)
        table_dst = sb("table_dst", [1, 2 * NG], i32)
        table_src = sb("table_src", [1, 2 * NG], i32)
        small = sb("small", [P, 64])
        tot = sb("tot", [P, NB])
        base = sb("base", [P, NB])
        start_of = sb("start_of", [P, NB])
        end_of = sb("end_of", [P, NB])
        stats = sb("stats", [P, NB, 6])
        mv = sb("mv", [P, NB, 2])
        rstd = sb("rstd", [P, NB])
        tT = sb("tT", [P, 2, 2 * P])
        one_f = sb("one_f", [P, 1])
        one_col = sb("one_col", [P, 1], bf16)
        zero_h = sb("zero_h", [P, P], bf16)
        wide, wide2, wide4 = (ctx.enter_context(nc.psum_tensor(n, [P, GE], f32)) for n in ("wide", "wide2", "wide4"))
        bank = [w[:, h * 512:(h + 1) * 512] for w in (wide, wide2, wide4) for h in range(2)]
        bank += [ctx.enter_context(nc.psum_tensor(f"bank{k}", [P, 512], f32)) for k in (6, 7)]

        sums_bank = bank[2]

        def A_(w):
            return A[:, 0:NB * w].rearrange("p (b f) -> p b f", f=w)

        Xv = X[:, :].rearrange("p (b f) -> p b f", f=F)
        z_table = dram("z_table", (NP_, ZW))
        x_tables = [dram(f"x_table{k}", (NP_, F)) for k in range(4)]
        sorted_rows = dram("sorted_rows", (EP, MW))
        range_dst = dram("range_dst", (NG, 2), i32)
        range_src = dram("range_src", (NG, 2), i32)

        DVE_RELS = N_RELS - POOL_RELS
        mask_pool, rel_pool = pos_i[:, :].bitcast(f32), cum

        def add_relation(e, r, marked, to, first):
            if first:
                e.tensor_scalar(to[:, :], type_f[:, :], float(r), rel_row[:, r:r + 1], ALU.is_equal, ALU.mult)
            else:
                e.tensor_scalar(marked[:, :], type_f[:, :], float(r), rel_row[:, r:r + 1], ALU.is_equal, ALU.mult)
                e.drain()
                e.tensor_tensor(to[:, :], to[:, :], marked[:, :], ALU.add)
                e.drain()

        s_small, s_edge, s_iota, s_w = sem("s_small"), sem("s_edge"), sem("s_iota"), sem("s_w")
        s_type = sem("s_type")
        s_gd, s_rng, s_rng_out, s_rng_in = sem("s_gd"), sem("s_rng"), sem("s_rng_out"), sem("s_rng_in")
        n_w = [0]
        gd = onehot[:, :, :].rearrange("p a b -> p (a b)").bitcast(i32)
        with nc.Block() as block:
            @block.sync
            def _(e):
                e.dma_start(consts[:, :], T["consts"][:, 0:C_SPREAD]).then_inc(s_small, 16)
                e.dma_start(onehot_t[0:PARTS * TILES, :], T["consts"][0:PARTS * TILES, C_SPREAD:C_WIDTH]
                            ).then_inc(s_small, 16)
                e.dma_start(src_i[:, :], T["src_c"]).then_inc(s_edge, 16)
                e.dma_start(dst_bc[:, 0, 0:GE], T["dst_row"][0:P, :]).then_inc(s_gd, 16)
                e.dma_start(dst_bc[0:NG - P, 1, 0:GE], T["dst_row"][P:NG, :]).then_inc(s_gd, 16)
                e.dma_start(X[:, :].rearrange("p (b f) -> p b f", f=F),
                            T["x"].rearrange("(b p) f -> p b f", p=P)).then_inc(s_edge, 16)
                e.dma_start(weight[:, :], T["weight_c"]).then_inc(s_edge, 16)
                e.dma_start(iota[:, :], T["iota"].to_broadcast([P, NP_])).then_inc(s_iota, 16)
                e.wait_ge(s_rng, 1)
                e.dma_start(range_dst[0:P, :], small[:, 4:6].bitcast(i32)).then_inc(s_rng_out, 16)
                e.dma_start(range_dst[P:NG, :], small[0:NG - P, 6:8].bitcast(i32)).then_inc(s_rng_out, 16)
                e.wait_ge(s_rng_out, 32)
                e.dma_start(table_dst[:, :], range_dst.rearrange("(a g) c -> a (g c)", a=1)).then_inc(s_rng_in, 16)
                e.wait_ge(s_rng_in, 16)
                e.wait_ge(s_iota, 16)

            @block.scalar
            def _(e):
                e.dma_start(type_f[:, :].bitcast(i32), T["type_c"]).then_inc(s_type, 16)
                e.dma_start(rel_row[:, :], T["rel_row"].to_broadcast([P, N_RELS])).then_inc(s_type, 16)
                e.dma_start(dst_f[:, :].bitcast(i32), T["dst_c"]).then_inc(s_edge, 16)
                for n in names:
                    e.dma_start(W[n][:, 0:F], T[n]).then_inc(s_w, 16)
                    n_w[0] += 16
                e.dma_start(attn[:, :], T["attn"]).then_inc(s_w, 16)
                e.dma_start(b1_col[:, :], T["b1_col"]).then_inc(s_w, 16)
                n_w[0] += 32
                for n in bias_names:
                    e.dma_start(bias[n][:, :], T[n].to_broadcast([P, F])).then_inc(s_w, 16)
                    n_w[0] += 16
                e.wait_ge(s_w, n_w[0])

            @block.vector
            def _(e):
                e.memset(one_col[:, :], 1.0)
                e.memset(zero_h[:, :], 0.0)
                e.memset(one_f[:, :], 1.0)
                e.wait_ge(s_small, 32)
                e.tensor_copy(ident_h[:, :], ident)
                e.tensor_copy(spread[:, :], onehot_t[0:PARTS * TILES, :])
                e.wait_ge(s_gd, 32)
                for c, rows_ in ((0, P), (1, NG - P)):
                    e.tensor_reduce(small[0:rows_, 2 * c:2 * c + 1], dst_bc[0:rows_, c, 0:GE], AX, ALU.min)
                    e.tensor_reduce(small[0:rows_, 2 * c + 1:2 * c + 2], dst_bc[0:rows_, c, 0:GE], AX, ALU.max)
                e.drain()
                for c, rows_ in ((0, P), (1, NG - P)):
                    e.tensor_scalar(small[0:rows_, 2 * c + 1:2 * c + 2], small[0:rows_, 2 * c + 1:2 * c + 2],
                                    float(P), None, ALU.add)
                e.drain()
                for c, rows_ in ((0, P), (1, NG - P)):
                    e.tensor_copy(small[0:rows_, 8 + 2 * c:10 + 2 * c].bitcast(i32), small[0:rows_, 2 * c:2 * c + 2])
                e.drain()
                for c, rows_ in ((0, P), (1, NG - P)):
                    ins = e.tensor_scalar(small[0:rows_, 4 + 2 * c:6 + 2 * c].bitcast(i32),
                                          small[0:rows_, 8 + 2 * c:10 + 2 * c].bitcast(i32), 7, None,
                                          ALU.arith_shift_right)
                ins.then_inc(s_rng, 1)
                e.wait_ge(s_type, 32)
                e.tensor_copy(type_f[:, :], type_f[:, :].bitcast(i32))
                e.drain()
                for r in range(EARLY_RELS):
                    add_relation(e, r, mask, rel, r == 0)
                e.wait_ge(s_edge, 64)
                e.tensor_copy(dst_f[:, :], dst_f[:, :].bitcast(i32))
                e.tensor_scalar(pos_i[:, :], src_i[:, :], 7, None, ALU.arith_shift_right)
                e.drain()
                e.tensor_copy(src_block[:, :], pos_i[:, :])
                e.drain()

        def node_products(tag, parts, w_out, finish, store=None):
            s_t, s_tc, s_o, s_f = sem(tag + "_t"), sem(tag + "_tc"), sem(tag + "_o"), sem(tag + "_f")
            k = len(parts)

            def run(block):
                @block.tensor
                def _(e):
                    def transposes(b):
                        if b >= 2:
                            e.wait_ge(s_tc, b - 1)
                        for n, (get, _) in enumerate(parts):
                            ins = e.matmul(wide[:, 512 * (b % 2) + n * P:512 * (b % 2) + (n + 1) * P], lhsT=get(b), rhs=ident,
                                           start=True, stop=True)
                        ins.then_inc(s_t, 1)

                    transposes(0)
                    for b in range(NB):
                        if b + 1 < NB:
                            transposes(b + 1)
                        e.wait_ge(s_tc, b + 1)
                        if b >= 2:
                            e.wait_ge(s_f, b - 1)
                        for n, (_, w) in enumerate(parts):
                            ins = e.matmul(bank[2 + b % 2][:, 0:w_out], lhsT=tT[:, b % 2, n * P:(n + 1) * P],
                                           rhs=w[:, 0:w_out], start=(n == 0), stop=(n == k - 1))
                        ins.then_inc(s_o, 1)

                @block.scalar
                def _(e):
                    for b in range(NB):
                        e.wait_ge(s_t, b + 1)
                        if b >= 2:
                            e.wait_ge(s_o, b - 1)
                        e.copy(tT[:, b % 2, 0:k * P], wide[:, 512 * (b % 2):512 * (b % 2) + k * P]).then_inc(s_tc, 1)

                @block.vector
                def _(e):
                    for b in range(NB):
                        e.wait_ge(s_o, b + 1)
                        finish(e, b, bank[2 + b % 2])
                        e.drain().then_inc(s_f, 1)
                    if store:
                        store(e)
            return run

        def layernorm(tag, to):
            s_v, s_sd, s_y, s_st = sem(tag + "_v"), sem(tag + "_sd"), sem(tag + "_y"), sem(tag + "_st")
            with nc.Block() as block:
                @block.vector
                def _(e):
                    for b in range(NB):
                        e.bn_stats(stats[:, b, :], Xv[:, b, :])
                    e.drain()
                    for b in range(NB):
                        e.bn_aggr(mv[:, b, :], stats[:, b, :])
                    e.drain()
                    e.tensor_scalar(rstd[:, :], mv[:, :, 1], EPS, None, ALU.add).then_inc(s_v, 1)
                    e.wait_ge(s_sd, 1)
                    e.reciprocal(rstd[:, :], rstd[:, :])
                    e.drain()
                    for b in range(NB):
                        e.tensor_scalar(Xv[:, b, :], Xv[:, b, :], mv[:, b, 0:1], rstd[:, b:b + 1],
                                        ALU.subtract, ALU.mult)
                    e.drain().then_inc(s_y, 1)

                @block.scalar
                def _(e):
                    e.wait_ge(s_v, 1)
                    e.activation(rstd[:, :], rstd[:, :], ACT.Sqrt).then_inc(s_sd, 1)

                @block.sync
                def _(e):
                    e.wait_ge(s_y, 1)
                    if to is not None:
                        store_nodes(e, to, Xv, s_st)

        def store_nodes(e, to, view, s_st):
            if to is out:
                full = N_NODES // P
                e.dma_start(out[0:full * P, :].rearrange("(b p) f -> p b f", p=P), view[:, 0:full, :]).then_inc(s_st, 16)
                e.dma_start(out[full * P:N_NODES, :], view[0:N_NODES - full * P, full, :]).then_inc(s_st, 16)
                e.wait_ge(s_st, 32)
            else:
                e.dma_start(to.rearrange("(b p) f -> p b f", p=P), view).then_inc(s_st, 16)
                e.wait_ge(s_st, 16)

        def range_registers(e, tag):
            return e.alloc_register(tag + "_first"), e.alloc_register(tag + "_end")

        def load_range(e, table, g, regs):
            e.load(list(regs), table[0:1, bass.ds(2 * g, 2)])

        def block_range(e, table, g, regs):
            load_range(e, table, g, regs)
            return same_range(e, regs)

        def same_range(e, regs):
            return (e.snap(regs[0], min_val=0, max_val=NB - 1), e.snap(regs[1], min_val=1, max_val=NB))

        def mark(e, s):
            e.matmul(bank[7][0:1, 0:1], lhsT=one_col[:, 0:1], rhs=one_col[:, 0:1], start=True, stop=True).then_inc(s, 1)

        def pe_sums(e, lo, hi, half_ready, half_done, group_rows, width, c):
            with e.Fori(lo, hi):
                e.reg_add(c, c, 1)
                for h in range(2):
                    e.wait_ge(half_ready[h], c)
                    for t in range(4 * h, 4 * h + 4):
                        ins = e.matmul(sums_bank[:, 0:width], lhsT=onehot[:, t, :], rhs=group_rows[:, t, 0:width],
                                       start=(t == 0), stop=(t == TILES - 1))
                    ins.then_inc(half_done[h], 1)

        def half_onehot(e, h, b, ids):
            return e.tensor_tensor(onehot[:, 4 * h:4 * h + 4, :],
                                   iota[:, bass.ds(b * P, P)].unsqueeze(1).to_broadcast([P, 4, P]),
                                   ids.to_broadcast([P, 4, P]), ALU.is_equal)

        def add_sums(e, b, width, scaled):
            to, new = A[:, bass.ds(b * width, width)], sums_bank[:, 0:width]
            if scaled:
                return e.scalar_tensor_tensor(out=to, in0=to, scalar=scale_now[:, 0:1], in1=new,
                                              op0=ALU.mult, op1=ALU.add)
            return e.tensor_tensor(to, to, new, ALU.add)

        def dve_sums_begin(e, tag, half_done, width):
            e.memset(A[:, 0:NB * width], 0.0)
            e.memset(sums_bank[:, :], 0.0)
            e.drain()
            for h in range(2):
                e.sem_inc(half_done[h], 1)
            last_b = e.alloc_register(tag + "_last_b")
            e.reg_mov(last_b, 0)
            return counter(e, tag + "_dve_pairs"), last_b

        def dve_sums(e, lo, hi, half_ready, half_done, ids_of, c, last_b, width, scale=None):
            with e.Fori(lo, hi) as b:
                e.reg_add(c, c, 1)
                before = e.snap(last_b)
                e.wait_ge(half_done[0], c)
                e.sem_inc(note["dve"], 1)
                half_onehot(e, 0, b, ids_of(0))
                e.wait_ge(half_done[1], c)
                e.sem_inc(note["dve"], 1)
                add_sums(e, before, width, scale is not None).then_inc(half_ready[0], 1)
                if scale is not None:
                    e.wait_ge(half_ready[0], c)
                    e.sem_inc(note["dve"], 1)
                    e.tensor_copy(scale_now[:, :], scale[:, bass.ds(b, 1)])
                half_onehot(e, 1, b, ids_of(1)).then_inc(half_ready[1], 1)
                e.reg_mov(last_b, b)

        def dve_sums_end(e, half_done, c, last_b, width, scaled=False):
            before = e.snap(last_b)
            e.reg_add(c, c, 1)
            e.wait_ge(half_done[1], c)
            e.sem_inc(note["dve"], 1)
            add_sums(e, before, width, scaled)
            e.drain()

        def counter(e, name, first=0):
            c = e.alloc_register(name)
            e.reg_mov(c, first)
            return c

        def gathers(tag, table, width, s_free):
            s_idx = sem(tag + "_idx")
            s_rows = [sem(f"{tag}_rows{s}") for s in range(SLOTS)]

            def run(block):
                @block.gpsimd
                def _(e):
                    with e.Fori(0, TURNS) as i:
                        for s in range(SLOTS):
                            e.wait_ge(s_free[s], i + 1)
                            e.tensor_copy(idx[:, s, :], src_i[:, bass.ds(i * (SLOTS * TILES) + s * TILES, TILES)]
                                          ).then_inc(s_idx, 1)
                            e.wait_ge(s_idx, i * SLOTS + (s + 1))
                            e.sem_inc(note["pool"], 1)
                            for t in range(TILES):
                                e.indirect_dma_start(
                                    out=rows[:, s, t, 0:width], out_offset=None, in_=table,
                                    in_offset=bass.IndirectOffsetOnAxis(ap=idx[:, s, t:t + 1], axis=0),
                                ).then_inc(s_rows[s], 16)
            return run, s_rows

        def load_dst_bc(e, s_free_, s_in):
            with e.Fori(0, TURNS) as i:
                for s in range(SLOTS):
                    k = s % 2
                    e.wait_ge(s_free_[k], i * 2 + (s // 2 + 1))
                    e.dma_start(dst_bc[:, k, :], T["dst_row"][bass.ds(i * SLOTS + s, 1), :].to_broadcast([P, GE])
                                ).then_inc(s_in[k], 16)

        note = {n: nc.alloc_semaphore(name="note_" + n) for n in ("dve", "pe", "act", "pool")}

        s_wa, s_wc, s_zst = sem("l0_wa"), sem("l0_wc"), sem("l0_zst")
        W0 = W["L0_gnn_Wt"]
        with nc.Block() as block:
            @block.tensor
            def _(e):
                e.matmul(bank[7][:, 0:2], lhsT=W["L0_gnn_W"][:, :], rhs=attn[:, :], start=True, stop=True
                         ).then_inc(s_wa, 1)

            @block.vector
            def _(e):
                e.wait_ge(s_wa, 1)
                e.tensor_copy(W0[:, F:F + 2], bank[7][:, 0:2]).then_inc(s_wc, 1)
                e.wait_ge(s_wc, 1)
        s_dst_n = sb("s_dst_n", [P, NB])
        far_node = sb("far_node", [P, NB])
        s_dst_p = sb("s_dst_p", [P, NB, PARTS], bf16)

        def finish_z(e, b, ps):
            e.tensor_copy(Z[:, b, 0:F + 2], ps[:, 0:F + 2])
            e.tensor_copy(s_dst_n[:, b:b + 1], ps[:, S_DST:S_DST + 1])
            if b < DVE_RELS - EARLY_RELS:
                add_relation(e, b + EARLY_RELS, mask, rel, False)

        Z = A_(ZW)
        Z_parts = A[:, 0:NB * ZW].bitcast(bf16).rearrange("p (b f) -> p b f", f=2 * ZW)[:, :, S_PARTS:S_PARTS + PARTS]
        assert DVE_RELS - EARLY_RELS <= NB
        run = node_products("l0z", [(lambda b: Xv[:, b, :], W0)], F + 2, finish_z)
        with nc.Block() as block:
            run(block)

            @block.gpsimd
            def _(e):
                for r in range(DVE_RELS, N_RELS):
                    add_relation(e, r, mask_pool, rel_pool, r == DVE_RELS)
        s_parts = sem("l0_parts")
        rest = sb("rest", [P, NB])
        with nc.Block() as block:
            @block.vector
            def _(e):
                e.tensor_copy(Z_parts[:, :, 0], Z[:, :, S_SRC])
                e.memset(Z_parts[:, :, 3], 0.0)
                e.drain()
                e.tensor_tensor(rest[:, :], Z[:, :, S_SRC], Z_parts[:, :, 0], ALU.subtract)
                e.drain()
                e.tensor_copy(Z_parts[:, :, 1], rest[:, :])
                e.drain()
                e.tensor_tensor(rest[:, :], rest[:, :], Z_parts[:, :, 1], ALU.subtract)
                e.drain()
                e.tensor_copy(Z_parts[:, :, 2], rest[:, :])
                e.drain().then_inc(s_parts, 1)
                e.tensor_tensor(rel[:, :], rel[:, :], rel_pool[:, :], ALU.add)
                e.tensor_copy(s_dst_p[:, :, 0], s_dst_n[:, :])
                e.tensor_scalar(far_node[:, :], node_id, -FAR, None, ALU.mult)
                e.drain()
                e.tensor_tensor(rest[:, :], s_dst_n[:, :], s_dst_p[:, :, 0], ALU.subtract)
                e.drain()
                e.tensor_copy(s_dst_p[:, :, 1], rest[:, :])
                e.drain()
                e.tensor_tensor(s_dst_p[:, :, 2], rest[:, :], s_dst_p[:, :, 1], ALU.subtract)
                e.drain()

            @block.sync
            def _(e):
                e.wait_ge(s_parts, 1)
                store_nodes(e, z_table, Z, s_zst)

        away = sb("away", [P, GE])
        onehot_th = onehot_t[:, 0:GE // 2].bitcast(bf16)
        hid = sb("hid", [P, GE])
        s_max = sb("s_max", [P, NB])
        m_node = sb("m_node", [P, NB])
        m_step = sb("m_step", [P, 2, NB])
        m_scale = sb("m_scale", [P, 2, NB])
        scale_now = sb("scale_now", [P, 1])
        q = sb("q", [P, 6], bf16)
        m_now = sb("m_now", [P, 3])
        look_all = sb("look_all", [P, TILES, 2])
        e_edge = sb("e_edge", [P, TILES])
        num = sb("num", [P, TILES])
        row_scale = sb("row_scale", [P, TILES])
        s_src_p = sb("s_src_p", [P, PARTS * TILES], bf16)
        s_src_t = sb("s_src_t", [PARTS * TILES, P], bf16)
        rows_h = rows[:, :, :, :].rearrange("p s t w -> p (s t w)").bitcast(bf16).rearrange(
            "p (s t w) -> p s t w", s=SLOTS, t=TILES)
        s_free = [sem(f"l0_free{s}") for s in range(SLOTS)]
        run_gather, s_rows = gathers("l0g", z_table, ZW, s_free)
        s_bc = [sem(f"l0_bc{k}") for k in range(2)]
        s_bcf = [sem(f"l0_bcf{k}") for k in range(2)]
        s_looked, s_ot, s_away, s_away_free, s_picked, s_turned, s_brought, s_sbc, s_q, s_look, s_ee, s_num, s_w_, s_scaled = (
            sem("l0_" + n) for n in ("looked", "ot", "away", "away_free", "picked", "turned", "brought", "sbc", "q", "look", "ee", "num", "w", "scaled"))
        half_ready, half_done = ([sem(f"l0_{n}{h}") for h in range(2)] for n in ("ready_half", "done_half"))
        look = bank[4][:, 0:6 * TILES]
        with nc.Block() as block:
            run_gather(block)

            @block.sync
            def _(e):
                load_dst_bc(e, s_bcf, s_bc)

            @block.scalar
            def _(e):
                def bring(g, i, s):
                    e.wait_ge(s_rows[s], (i + 1) * 16 * TILES)
                    e.sem_inc(note["act"], 1)
                    e.copy(s_src_p[:, :].rearrange("p (t k) -> p t k", k=PARTS),
                           rows_h[:, s, :, S_PARTS:S_PARTS + PARTS]).then_inc(s_picked, 1)
                    e.wait_ge(s_turned, g + 1)
                    e.sem_inc(note["act"], 1)
                    e.copy(s_src_t[:, :], bank[5][0:PARTS * TILES, 0:P]).then_inc(s_brought, 1)

                def scale_rows(g, s):
                    e.wait_ge(s_w_, g + 1)
                    e.sem_inc(note["act"], 1)
                    for t in range(TILES):
                        ins = e.activation(rows[:, s, t, 0:F], rows[:, s, t, 0:F], ACT.Copy,
                                           scale=row_scale[:, t:t + 1])
                    ins.then_inc(s_scaled, 1)

                c = counter(e, "l0_act_pairs", 1)
                regs = range_registers(e, "l0_act")
                before = e.alloc_register("l0_act_before")
                for k in range(2):
                    e.sem_inc(s_bcf[k], 1)
                e.reg_mov(before, 0)
                for first in (s_away, s_ot, s_q, s_look, s_away_free, s_away_free):
                    e.sem_inc(first, 1)
                bring(0, 0, 0)
                with e.Fori(0, TURNS) as i:
                    for s in range(SLOTS):
                        g, k = i * SLOTS + s, s % 2
                        lo, hi = block_range(e, table_dst, g, regs)
                        e.wait_ge(s_bc[k], (i * 2 + (s // 2 + 1)) * 16)
                        e.sem_inc(note["act"], 1)
                        with e.Fori(lo, hi) as b:
                            e.wait_ge(s_ot, c)
                            e.wait_ge(s_look, c)
                            e.reg_add(c, c, 1)
                            e.wait_ge(s_away_free, c)
                            e.sem_inc(note["act"], 1)
                            e.activation(away[:, :], dst_bc[:, k, :], ACT.Square, scale=FAR,
                                         bias=far_node[:, bass.ds(b, 1)]).then_inc(s_away, 1)
                            e.wait_ge(s_away, c)
                            e.sem_inc(note["act"], 1)
                            ins = e.activation(onehot_th, away[:, :], ACT.Relu, scale=-1.0, bias=one_f[:, 0:1])
                            ins.then_inc(s_ot, 1)
                        e.drain().then_inc(s_bcf[k], 1)
                        if s:
                            scale_rows(g - 1, s - 1)
                        else:
                            with e.If(i > 0):
                                scale_rows(e.snap(before, min_val=0, max_val=NG - 1), SLOTS - 1)
                        if s < SLOTS - 1:
                            bring(g + 1, i, s + 1)
                        else:
                            with e.If(i < TURNS - 1):
                                bring(g + 1, i + 1, 0)
                        e.wait_ge(s_ee, g + 2)
                        e.sem_inc(note["act"], 1)
                        e.activation(num[:, :], e_edge[:, :], ACT.Exp)
                        e.activation(m_scale[:, k, :], m_step[:, k, :], ACT.Exp).then_inc(s_num, 1)
                    e.reg_mov(before, i * SLOTS + (SLOTS - 1))
                scale_rows(NG - 1, SLOTS - 1)

            @block.tensor
            def _(e):
                c = counter(e, "l0_pe_looks", 1)
                c2 = counter(e, "l0_pe_pairs")
                regs = [range_registers(e, f"l0_pe{s}") for s in range(SLOTS)]
                ranges = [None] * SLOTS
                e.reg_mov(regs[-1][0], 0)
                e.reg_mov(regs[-1][1], 1)
                before = e.alloc_register("l0_pe2_before")
                e.reg_mov(before, 0)

                def spread_s(g):
                    e.wait_ge(s_picked, g + 1)
                    e.sem_inc(note["pe"], 1)
                    e.matmul(bank[5][0:PARTS * TILES, 0:P], lhsT=s_src_p[:, :],
                             rhs=ident_h[:, :], start=True, stop=True).then_inc(s_turned, 1)
                    e.wait_ge(s_brought, g + 1)
                    e.sem_inc(note["pe"], 1)
                    for t in range(TILES):
                        ins = e.matmul(wide[:, t * P:(t + 1) * P],
                                       lhsT=spread[:, t * P:(t + 1) * P], rhs=s_src_t[:, :], start=True, stop=True)
                    ins.then_inc(s_sbc, 1)

                def sums(g, s, lo, hi):
                    e.wait_ge(s_scaled, g + 1)
                    e.sem_inc(note["pe"], 1)
                    pe_sums(e, lo, hi, half_ready, half_done, rows[:, s, :, :], MW, c2)
                    mark(e, s_free[s])

                for s in range(SLOTS):
                    e.sem_inc(s_free[s], 1)
                spread_s(0)
                with e.Fori(0, TURNS) as i:
                    for s in range(SLOTS):
                        g = i * SLOTS + s
                        ranges[s] = lo, hi = block_range(e, table_dst, g, regs[s])
                        e.wait_ge(s_ee, g + 1)
                        e.sem_inc(note["pe"], 1)
                        e.matmul(look, lhsT=zero_h[0:1, :], rhs=zero_h[0:1, 0:6 * TILES], start=True, stop=False)
                        with e.Fori(lo, hi):
                            e.reg_add(c, c, 1)
                            e.wait_ge(s_ot, c)
                            e.wait_ge(s_q, c)
                            e.sem_inc(note["pe"], 1)
                            for t in range(TILES):
                                ins = e.matmul(look[:, 6 * t:6 * t + 6], lhsT=onehot_th[:, t * P:(t + 1) * P],
                                               rhs=q[:, :], start=False, stop=False)
                            ins.then_inc(s_look, 1)
                        e.matmul(look[:, 0:1], lhsT=zero_h[0:1, :], rhs=zero_h[0:1, 0:1], start=False, stop=True
                                 ).then_inc(s_looked, 1)
                        if s < SLOTS - 1:
                            spread_s(g + 1)
                        else:
                            with e.If(i < TURNS - 1):
                                spread_s(g + 1)
                        if s:
                            sums(g - 1, s - 1, *ranges[s - 1])
                        else:
                            with e.If(i > 0):
                                sums(e.snap(before, min_val=0, max_val=NG - 1), SLOTS - 1, *same_range(e, regs[-1]))
                    e.reg_mov(before, i * SLOTS + (SLOTS - 1))
                sums(NG - 1, SLOTS - 1, *same_range(e, regs[-1]))

            @block.vector
            def _(e):
                e.memset(s_max[:, :], -HUGE)
                e.memset(m_node[:, :], -HUGE * SLOPE)
                e.memset(m_step[:, :, :], 0.0)
                e.memset(scale_now[:, :], 1.0)
                c2, last_b = dve_sums_begin(e, "l0", half_done, MW)
                c = counter(e, "l0_dve_looks", 1)
                c_last = counter(e, "l0_dve_last_look", 1)
                e.sem_inc(s_ee, 1)
                regs = [range_registers(e, f"l0_dve{s}") for s in range(SLOTS)]
                ranges = [None] * SLOTS
                e.reg_mov(regs[-1][0], 0)
                e.reg_mov(regs[-1][1], 1)
                before = e.alloc_register("l0_dve2_before")
                e.reg_mov(before, 0)
                def sums(g, k, lo, hi):
                    dve_sums(e, lo, hi, half_ready, half_done,
                             lambda h: dst_f[:, bass.ds(g * TILES + 4 * h, 4)].unsqueeze(2), c2, last_b, MW,
                             m_scale[:, k, :])

                with e.Fori(0, TURNS) as i:
                    for s in range(SLOTS):
                        g, k = i * SLOTS + s, s % 2
                        if s == 0:
                            load_range(e, table_dst, g, regs[0])
                        ranges[s] = lo, hi = same_range(e, regs[s])
                        with e.Fori(lo, hi) as b:
                            e.reg_add(c, c, 1)
                            e.tensor_copy(small[:, 16:17], s_max[:, bass.ds(b, 1)])
                            e.drain()
                            e.wait_ge(s_away, c)
                            e.wait_ge(s_sbc, g + 1)
                            e.sem_inc(note["dve"], 1)
                            e.tensor_tensor_reduce(out=hid[:, :], in0=wide[:, :], in1=away[:, :], scale=1.0,
                                                   scalar=small[:, 16:17], op0=ALU.subtract, op1=ALU.max,
                                                   accum_out=small[:, 17:18])
                            e.tensor_copy(m_now[:, 1:2], s_dst_n[:, bass.ds(b, 1)])
                            e.wait_ge(s_look, c_last)
                            e.sem_inc(note["dve"], 1)
                            e.tensor_copy(q[:, 0:3], s_dst_p[:, bass.ds(b, 1), 0:3].rearrange("p a k -> p (a k)"))
                            if s < SLOTS - 1:
                                load_range(e, table_dst, g + 1, regs[s + 1])
                            e.drain().then_inc(s_away_free, 1)
                            e.tensor_tensor(small[:, 19:20], small[:, 17:18], m_now[:, 1:2], ALU.add)
                            e.drain()
                            for m_to in (m_now[:, 0:1], q[:, 3:4]):
                                e.scalar_tensor_tensor(out=m_to, in0=small[:, 19:20], scalar=SLOPE,
                                                       in1=small[:, 19:20], op0=ALU.mult, op1=ALU.max)
                            e.drain()
                            for m_rest in (m_now[:, 1:2], q[:, 4:5]):
                                e.tensor_tensor(m_rest, m_now[:, 0:1], q[:, 3:4], ALU.subtract)
                            e.drain()
                            e.tensor_tensor(q[:, 5:6], m_now[:, 1:2], q[:, 4:5], ALU.subtract).then_inc(s_q, 1)
                            e.tensor_copy(s_max[:, bass.ds(b, 1)], small[:, 17:18])
                            e.tensor_tensor(m_step[:, k, bass.ds(b, 1)], m_node[:, bass.ds(b, 1)], m_now[:, 0:1],
                                            ALU.subtract)
                            e.drain()
                            e.tensor_copy(m_node[:, bass.ds(b, 1)], m_now[:, 0:1])
                            e.reg_add(c_last, c_last, 1)
                        e.drain()
                        e.wait_ge(s_looked, g + 1)
                        e.sem_inc(note["dve"], 1)
                        e.tensor_reduce(look_all[:, :, :].rearrange("p t c -> p (t c)"),
                                        look.rearrange("p (n k) -> p n k", k=3), AX, ALU.add)
                        e.drain()
                        e.tensor_tensor(e_edge[:, :], rows[:, s, :, S_SRC], look_all[:, :, 0], ALU.add)
                        e.drain()
                        e.scalar_tensor_tensor(out=e_edge[:, :], in0=e_edge[:, :], scalar=SLOPE, in1=e_edge[:, :],
                                               op0=ALU.mult, op1=ALU.max)
                        e.drain()
                        e.tensor_tensor(e_edge[:, :], e_edge[:, :], look_all[:, :, 1], ALU.subtract).then_inc(s_ee, 1)
                        if s:
                            sums(g - 1, 1 - k, *ranges[s - 1])
                        else:
                            with e.If(i > 0):
                                sums(e.snap(before, min_val=0, max_val=NG - 1), 1 - k, *same_range(e, regs[-1]))
                        e.wait_ge(s_num, g + 1)
                        e.sem_inc(note["dve"], 1)
                        e.tensor_copy(rows[:, s, :, F], num[:, :])
                        e.tensor_tensor(row_scale[:, :], num[:, :], rel[:, bass.ds(g * TILES, TILES)], ALU.mult
                                        ).then_inc(s_w_, 1)
                    e.reg_mov(before, i * SLOTS + (SLOTS - 1))
                sums(NG - 1, (NG - 1) % 2, *same_range(e, regs[-1]))
                dve_sums_end(e, half_done, c2, last_b, MW, True)

        rden = sb("rden", [P, NB])
        A0 = A_(MW)
        with nc.Block() as block:
            @block.vector
            def _(e):
                e.tensor_scalar(rden[:, :], A0[:, :, F], TINY, None, ALU.max)
                e.drain()
                e.reciprocal(rden[:, :], rden[:, :])
                e.drain()
                for b in range(NB):
                    e.scalar_tensor_tensor(out=Xv[:, b, :], in0=A0[:, b, 0:F], scalar=rden[:, b:b + 1],
                                           in1=Xv[:, b, :], op0=ALU.mult, op1=ALU.add)
                e.drain()
                e.tensor_tensor(Xv, Xv, bias["L0_gnn_bias_w"][:, :].unsqueeze(1).to_broadcast([P, NB, F]), ALU.add)
                e.memset(rows[:, :, :, F], 1.0)
                e.drain()
        layernorm("l0n", x_tables[0])
        release_semaphores()

        def sum_pass(tag, table, weighted, extra):
            width = F if weighted else MW
            s_free = [sem(f"{tag}_free{s}") for s in range(SLOTS)]
            run_gather, s_rows = gathers(tag, table, F, s_free)
            s_ready = [sem(f"{tag}_ready{s}") for s in range(SLOTS)]
            half_ready, half_done = ([sem(f"{tag}_{n}{h}") for h in range(2)] for n in ("ready_half", "done_half"))
            with nc.Block() as block:
                run_gather(block)
                if weighted:
                    @block.scalar
                    def _(e):
                        with e.Fori(0, TURNS) as i:
                            for s in range(SLOTS):
                                e.wait_ge(s_rows[s], (i + 1) * 16 * TILES)
                                e.sem_inc(note["act"], 1)
                                for t in range(TILES):
                                    ins = e.activation(
                                        rows[:, s, t, 0:F], rows[:, s, t, 0:F], ACT.Copy,
                                        scale=weight[:, bass.ds(i * (SLOTS * TILES) + (s * TILES + t), 1)])
                                ins.then_inc(s_ready[s], 1)

                @block.tensor
                def _(e):
                    c = counter(e, tag + "_pe_pairs")
                    regs = range_registers(e, tag + "_pe")
                    for s in range(SLOTS):
                        e.sem_inc(s_free[s], 1)
                    with e.Fori(0, TURNS) as i:
                        for s in range(SLOTS):
                            lo, hi = block_range(e, table_dst, i * SLOTS + s, regs)
                            if weighted:
                                e.wait_ge(s_ready[s], i + 1)
                            else:
                                e.wait_ge(s_rows[s], (i + 1) * 16 * TILES)
                            e.sem_inc(note["pe"], 1)
                            pe_sums(e, lo, hi, half_ready, half_done, rows[:, s, :, :], width, c)
                            mark(e, s_free[s])

                @block.vector
                def _(e):
                    c, last_b = dve_sums_begin(e, tag, half_done, width)
                    regs = range_registers(e, tag + "_dve")
                    with e.Fori(0, TURNS) as i:
                        if extra:
                            extra(e, i)
                        for s in range(SLOTS):
                            g = i * SLOTS + s
                            lo, hi = block_range(e, table_dst, g, regs)
                            dve_sums(e, lo, hi, half_ready, half_done,
                                     lambda h: dst_f[:, bass.ds(g * TILES + 4 * h, 4)].unsqueeze(2), c, last_b, width)
                    dve_sums_end(e, half_done, c, last_b, width)

        def count_bucket(e, i):
            e.tensor_scalar(mask[:, :], src_block[:, :], iota[:, bass.ds(i, 1)], None, ALU.is_equal)
            e.drain()
            e.tensor_reduce(tot[:, bass.ds(i, 1)], mask[:, :], AX, ALU.add)

        def place_bucket(e, i):
            e.tensor_scalar(mask[:, :], src_block[:, :], iota[:, bass.ds(i, 1)], None, ALU.is_equal)
            e.tensor_copy(small[:, 20:21], base[:, bass.ds(i, 1)])
            e.drain()
            e.tensor_tensor_scan(cum[:, :], mask[:, :], mask[:, :], small[:, 20:21], ALU.add, ALU.max)
            e.drain()
            e.copy_predicated(pos[:, :], mask[:, :].bitcast(u32), cum[:, :])
            e.drain()

        sum_pass("l1", x_tables[0], False, count_bucket)

        s_tot, s_ps, s_base, s_ro, s_ri = sem("so_tot"), sem("so_ps"), sem("so_base"), sem("so_ro"), sem("so_ri")
        with nc.Block() as block:
            @block.tensor
            def _(e):
                e.matmul(bank[4][:, 0:NB], lhsT=tri, rhs=tot[:, :], start=True, stop=True)
                e.matmul(bank[5][:, 0:NB], lhsT=ones, rhs=tot[:, :], start=True, stop=True).then_inc(s_ps, 1)

            @block.vector
            def _(e):
                e.wait_ge(s_ps, 1)
                e.tensor_copy(tot[:, :], bank[5][:, 0:NB])
                e.drain()
                e.tensor_tensor_scan(end_of[:, :], tot[:, :], tot[:, :], 0.0, ALU.add, ALU.max)
                e.drain()
                e.tensor_tensor(start_of[:, :], end_of[:, :], bank[5][:, 0:NB], ALU.subtract)
                e.drain()
                e.tensor_tensor(base[:, :], start_of[:, :], bank[4][:, 0:NB], ALU.add)
                for c in range(2):
                    e.tensor_scalar(cum[:, 0:NB], end_of[:, :], group_at[:, c:c + 1], None, ALU.is_le)
                    e.tensor_scalar(mask[:, 0:NB], start_of[:, :], group_at[:, c:c + 1], float(GE - 1),
                                    ALU.subtract, ALU.is_le)
                    e.drain()
                    e.tensor_reduce(small[:, 24 + 2 * c:25 + 2 * c], cum[:, 0:NB], AX, ALU.add)
                    e.tensor_reduce(small[:, 25 + 2 * c:26 + 2 * c], mask[:, 0:NB], AX, ALU.add)
                    e.drain()
                    ins = e.tensor_copy(small[:, 28 + 2 * c:30 + 2 * c].bitcast(i32), small[:, 24 + 2 * c:26 + 2 * c])
                    e.drain()
                e.drain().then_inc(s_base, 1)

            @block.sync
            def _(e):
                e.wait_ge(s_base, 1)
                for c in range(2):
                    e.dma_start(range_src[c * HG:(c + 1) * HG, :], small[0:HG, 28 + 2 * c:30 + 2 * c].bitcast(i32)
                                ).then_inc(s_ro, 16)
                e.wait_ge(s_ro, 32)
                e.dma_start(table_src[:, :], range_src.rearrange("(a g) c -> a (g c)", a=1)).then_inc(s_ri, 16)
                e.wait_ge(s_ri, 16)

        A1 = A_(MW)
        with nc.Block() as block:
            @block.vector
            def _(e):
                e.tensor_scalar(rden[:, :], A1[:, :, F], 1.0, None, ALU.max)
                e.drain()
                e.reciprocal(rden[:, :], rden[:, :])
                e.drain()
                for b in range(NB):
                    e.tensor_scalar(A1[:, b, 0:F], A1[:, b, 0:F], rden[:, b:b + 1], None, ALU.mult)
                e.drain()

        def add_to_x(e, b, ps):
            e.tensor_tensor(Xv[:, b, :], Xv[:, b, :], ps[:, 0:F], ALU.add)

        run = node_products("l1d", [(lambda b: A1[:, b, 0:F], W["L1_gnn_W_lt"]), (lambda b: Xv[:, b, :], W["L1_gnn_W_rt"])],
                            F, add_to_x)
        with nc.Block() as block:
            run(block)
        layernorm("l1n", x_tables[1])
        release_semaphores()

        A2 = A_(F)
        Hv = H[:, :].rearrange("p (b f) -> p b f", f=F)
        for k in range(3):
            sum_pass(f"l2{k}", x_tables[1 + k] if k < 2 else x_tables[3], True, place_bucket if k == 0 else None)
            b_row = bias[f"L2_gnn_b_rel{k + 1}"]

            def finish_conv(e, b, ps, k=k, b_row=b_row):
                if k < 2:
                    e.tensor_tensor(Hv[:, b, :], ps[:, 0:F], b_row[:, :], ALU.add)
                    e.drain()
                    e.tensor_scalar(Hv[:, b, :], Hv[:, b, :], 0.0, None, ALU.max)
                else:
                    e.tensor_tensor(Xv[:, b, :], Xv[:, b, :], ps[:, 0:F], ALU.add)
                    e.drain()
                    e.tensor_tensor(Xv[:, b, :], Xv[:, b, :], b_row[:, :], ALU.add)

            own = Xv if k == 0 else Hv
            run = node_products(f"l2d{k}", [(lambda b: A2[:, b, :], W[f"L2_gnn_W_rel{k + 1}t"]),
                                            (lambda b, own=own: own[:, b, :], W[f"L2_gnn_W_root{k + 1}t"])],
                                F, finish_conv)
            with nc.Block() as block:
                run(block)
            if k < 2:
                s_hst = sem(f"l2_hst{k}")
                with nc.Block() as block:
                    @block.sync
                    def _(e):
                        store_nodes(e, x_tables[2 + k], Hv, s_hst)
        layernorm("l2n", None)
        release_semaphores()

        h_high, h_middle = (H[:, :].bitcast(bf16)[:, k * NB * F:(k + 1) * NB * F] for k in range(2))
        h_low = dst_weight[:, :].bitcast(bf16)
        h_parts = (h_high, h_middle, h_low)
        SPLIT = 7
        assert NB % SPLIT == 0 and 2 * NG * TILES * 2 == NB * F

        def finish_h(e, b, ps):
            e.tensor_tensor(A[:, b * F:(b + 1) * F], ps[:, 0:F], bias["L3_gnn_bl"][:, :], ALU.add)
            if b % SPLIT == SPLIT - 1:
                c = slice((b + 1 - SPLIT) * F, (b + 1) * F)
                e.drain()
                e.tensor_copy(h_high[:, c], A[:, c])
                e.drain()
                e.tensor_tensor(A[:, c], A[:, c], h_high[:, c], ALU.subtract)
                e.drain()
                e.tensor_copy(h_middle[:, c], A[:, c])
                e.drain()
                e.tensor_tensor(h_low[:, c], A[:, c], h_middle[:, c], ALU.subtract)

        s_pos = sem("s_pos")
        run = node_products("l3h", [(lambda b: Xv[:, b, :], W["L3_gnn_Wl"])], F, finish_h)
        with nc.Block() as block:
            run(block)

            @block.gpsimd
            def _(e):
                e.tensor_scalar(pos[:, :], pos[:, :], -1.0, None, ALU.add).then_inc(s_pos, 1)
                e.wait_ge(s_pos, 1)
                e.tensor_copy(pos_i[:, :], pos[:, :]).then_inc(s_pos, 1)
                e.wait_ge(s_pos, 2)

        b2_rows = sb("b2_rows", [P, 4 * F], bf16)
        ones_h = sb("ones_h", [P, P], bf16)
        with nc.Block() as block:
            @block.vector
            def _(e):
                b2 = bias["L3_gnn_b2"]
                part, left, picked = onehot_t[:, 0:F // 2].bitcast(bf16), onehot_t[:, F:2 * F], onehot_t[:, 2 * F:3 * F]
                e.memset(ones_h[:, :], 1.0)
                e.tensor_copy(left, b2[:, :])
                e.memset(picked, 0.0)
                e.drain()
                for k in range(3):
                    e.tensor_copy(part, left)
                    e.drain()
                    e.scalar_tensor_tensor(out=picked, in0=part, scalar=ident[:, k:k + 1], in1=picked,
                                           op0=ALU.mult, op1=ALU.add)
                    e.tensor_tensor(left, left, part, ALU.subtract)
                    e.drain()
                for t in range(4):
                    e.tensor_copy(b2_rows[:, t * F:(t + 1) * F], picked)
                e.drain()

        attr = onehot[:, :, :].rearrange("p (k t) n -> p k (t n)", k=2)
        filters, h_dst, h_sb = wide2, wide4, away
        s_bc = [sem(f"l3_bc{k}") for k in range(2)]
        s_bcf = [sem(f"l3_bcf{k}") for k in range(2)]
        s_at = [sem(f"l3_at{k}") for k in range(2)]
        s_atf = [sem(f"l3_atf{k}") for k in range(2)]
        s_h, s_hs, s_msg, s_mm1, s_hid, s_mm2, s_read, s_ot, s_look, s_idx, s_nt = (
            sem("l3_" + n) for n in ("h", "hs", "msg", "mm1", "hid", "mm2", "read", "ot", "look", "idx", "nt"))
        s_scat = [sem(f"l3_scat{s}") for s in range(SLOTS)]
        with nc.Block() as block:
            @block.sync
            def _(e):
                with e.Fori(0, TURNS) as i:
                    for s in range(SLOTS):
                        k = s % 2
                        e.wait_ge(s_bcf[k], i * 2 + (s // 2 + 1))
                        e.dma_start(dst_bc[:, k, :], T["dst_row"][bass.ds(i * SLOTS + s, 1), :].to_broadcast([P, GE])
                                    ).then_inc(s_bc[k], 16)
                        e.wait_ge(s_atf[k], i * 2 + (s // 2 + 1))
                        e.dma_start(attr[:, k, :], T["attr_t"][bass.ds(i * SLOTS + s, 1), :, :].rearrange(
                            "a p n -> (a p) n")).then_inc(s_at[k], 16)

            @block.tensor
            def _(e):
                c = counter(e, "l3_pe_looks", 1)
                regs = range_registers(e, "l3_pe")

                def hidden(i, s):
                    k = s % 2
                    e.wait_ge(s_at[k], (i * 2 + (s // 2 + 1)) * 16)
                    e.sem_inc(s_nt, 1)
                    for h in range(2):
                        r = slice(h * N_RBF, (h + 1) * N_RBF)
                        ins = e.matmul(wide[:, h * 512:(h + 1) * 512], lhsT=W["L3_gnn_W1d"][r, 0:F], rhs=attr[r, k, :],
                                       start=True, stop=True)
                    ins.then_inc(s_mm1, 1)
                    mark(e, s_atf[k])

                def lookup(b, first):
                    e.reg_add(c, c, 1)
                    e.wait_ge(s_ot, c)
                    e.sem_inc(s_nt, 1)
                    for t in range(TILES):
                        for k, part in enumerate(h_parts):
                            ins = e.matmul(h_dst[:, t * P:(t + 1) * P], lhsT=onehot_th[:, t * P:(t + 1) * P],
                                           rhs=part[:, bass.ds(b * F, F)], start=(first and k == 0 and t % 4 == 0), stop=False)
                    ins.then_inc(s_look, 1)

                for k in range(2):
                    e.sem_inc(s_atf[k], 1)
                hidden(0, 0)
                with e.Fori(0, TURNS) as i:
                    for s in range(SLOTS):
                        g = i * SLOTS + s
                        lo, hi = block_range(e, table_dst, g, regs)
                        e.wait_ge(s_read, g + 1)
                        e.sem_inc(s_nt, 1)
                        lookup(hi - 1, True)
                        with e.If(hi - lo > 1):
                            with e.Fori(lo, hi - 1) as b:
                                lookup(b, False)
                        for h in range(2):
                            ins = e.matmul(h_dst[:, h * 512:h * 512 + 1], lhsT=zero_h[0:1, :], rhs=one_col[0:1, :],
                                           start=False, stop=True)
                        ins.then_inc(s_h, 1)
                        for h in range(2):
                            e.matmul(filters[:, h * 512:(h + 1) * 512], lhsT=ones_h[0:3, :], rhs=b2_rows[0:3, :],
                                     start=True, stop=False)
                        e.wait_ge(s_hid, g + 1)
                        e.sem_inc(s_nt, 1)
                        for t in range(TILES):
                            ins = e.matmul(filters[:, t * P:(t + 1) * P], lhsT=hid[:, t * P:(t + 1) * P],
                                           rhs=W["L3_gnn_W2"][:, :], start=False, stop=(t % 4 == 3))
                        ins.then_inc(s_mm2, 1)
                        if s < SLOTS - 1:
                            hidden(i, s + 1)
                        else:
                            with e.If(i < TURNS - 1):
                                hidden(i + 1, 0)

            @block.scalar
            def _(e):
                e.sem_inc(s_read, 1)
                with e.Fori(0, NG) as g:
                    e.wait_ge(s_mm1, g + 1)
                    e.sem_inc(note["act"], 1)
                    e.activation(hid[:, :], wide[:, :], ACT.Relu, bias=b1_col[:, 0:1]).then_inc(s_hid, 1)
                    e.wait_ge(s_read, g + 1)
                    e.wait_ge(s_h, g + 1)
                    e.sem_inc(note["act"], 1)
                    e.copy(h_sb[:, :], h_dst[:, :]).then_inc(s_hs, 1)

            @block.vector
            def _(e):
                c = counter(e, "l3_dve_looks", 1)
                regs = range_registers(e, "l3_dve")
                before = e.alloc_register("l3_dve_before")
                e.reg_mov(before, 0)

                def onehot_of(b, k):
                    e.wait_ge(s_look, c)
                    e.reg_add(c, c, 1)
                    e.sem_inc(s_nt, 1)
                    e.tensor_scalar(onehot_th, dst_bc[:, k, :], node_id[:, bass.ds(b, 1)], None, ALU.is_equal
                                    ).then_inc(s_ot, 1)

                def messages(i, s):
                    g = i * SLOTS + s
                    e.wait_ge(s_mm2, g + 1)
                    e.sem_inc(s_nt, 1)
                    with e.If(i > 0):
                        e.wait_ge(s_scat[s], i * (16 * TILES))
                        e.sem_inc(s_nt, 1)
                    e.sem_inc(s_nt, 1)
                    e.wait_ge(s_hs, g + 1)
                    e.sem_inc(s_nt, 1)
                    e.tensor_tensor(rows[:, s, :, 0:F], filters[:, :].rearrange("p (t f) -> p t f", f=F),
                                    h_sb[:, :].rearrange("p (t f) -> p t f", f=F), ALU.mult).then_inc(s_read, 1)
                    e.tensor_copy(rows[:, s, :, F], src_i[:, bass.ds(g * TILES, TILES)]).then_inc(s_msg, 1)

                for k in range(2):
                    e.sem_inc(s_bcf[k], 1)
                for first in (s_look, s_ot):
                    e.sem_inc(first, 1)
                with e.Fori(0, TURNS) as i:
                    for s in range(SLOTS):
                        g, k = i * SLOTS + s, s % 2
                        lo, hi = block_range(e, table_dst, g, regs)
                        e.wait_ge(s_bc[k], (i * 2 + (s // 2 + 1)) * 16)
                        e.sem_inc(s_nt, 1)
                        onehot_of(hi - 1, k)
                        if s:
                            messages(i, s - 1)
                        else:
                            with e.If(i > 0):
                                messages(e.snap(before, min_val=0, max_val=TURNS - 1), SLOTS - 1)
                        with e.If(hi - lo > 1):
                            with e.Fori(lo, hi - 1) as b:
                                onehot_of(b, k)
                        e.drain().then_inc(s_bcf[k], 1)
                    e.reg_mov(before, i)
                messages(e.snap(before, min_val=0, max_val=TURNS - 1), SLOTS - 1)

            @block.gpsimd
            def _(e):
                with e.Fori(0, TURNS) as i:
                    for s in range(SLOTS):
                        e.wait_ge(s_msg, i * SLOTS + (s + 1))
                        e.tensor_copy(idx[:, s, :], pos_i[:, bass.ds(i * (SLOTS * TILES) + s * TILES, TILES)]
                                      ).then_inc(s_idx, 1)
                        e.wait_ge(s_idx, i * SLOTS + (s + 1))
                        e.sem_inc(s_nt, 1)
                        for t in range(TILES):
                            e.indirect_dma_start(
                                out=sorted_rows, out_offset=bass.IndirectOffsetOnAxis(ap=idx[:, s, t:t + 1], axis=0),
                                in_=rows[:, s, t, 0:MW], in_offset=None).then_inc(s_scat[s], 16)
                for s in range(SLOTS):
                    e.wait_ge(s_scat[s], TURNS * 16 * TILES)

        s_in = [sem(f"l3_in{s}") for s in range(SLOTS)]
        s_inf = [sem(f"l3_inf{s}") for s in range(SLOTS)]
        half_ready, half_done = ([sem(f"l3b_{n}{h}") for h in range(2)] for n in ("ready_half", "done_half"))
        msgs = [rows[:, s, :, :].rearrange("p t w -> p (t w)")[:, 0:TILES * MW] for s in range(SLOTS)]
        sorted_v = sorted_rows.rearrange("(g p t) w -> g p (t w)", p=P, t=TILES)
        with nc.Block() as block:
            @block.sync
            def _(e):
                with e.Fori(0, TURNS) as i:
                    for s in range(SLOTS):
                        e.wait_ge(s_inf[s], i + 1)
                        e.dma_start(msgs[s], sorted_v[bass.ds(i * SLOTS + s, 1), :, :].rearrange("a p n -> (a p) n")
                                    ).then_inc(s_in[s], 16)

            @block.tensor
            def _(e):
                c = counter(e, "l3b_pe_pairs")
                regs = range_registers(e, "l3b_pe")
                for s in range(SLOTS):
                    e.sem_inc(s_inf[s], 1)
                with e.Fori(0, TURNS) as i:
                    for s in range(SLOTS):
                        lo, hi = block_range(e, table_src, i * SLOTS + s, regs)
                        e.wait_ge(s_in[s], (i + 1) * 16)
                        e.sem_inc(note["pe"], 1)
                        pe_sums(e, lo, hi, half_ready, half_done, msgs[s].rearrange("p (t w) -> p t w", w=MW), F, c)
                        mark(e, s_inf[s])

            @block.vector
            def _(e):
                c, last_b = dve_sums_begin(e, "l3b", half_done, F)
                regs = range_registers(e, "l3b_dve")
                with e.Fori(0, TURNS) as i:
                    for s in range(SLOTS):
                        lo, hi = block_range(e, table_src, i * SLOTS + s, regs)
                        e.wait_ge(s_in[s], (i + 1) * 16)
                        e.sem_inc(note["dve"], 1)
                        mv_ = msgs[s].rearrange("p (t w) -> p t w", w=MW)
                        dve_sums(e, lo, hi, half_ready, half_done, lambda h: mv_[:, 4 * h:4 * h + 4, F:F + 1], c, last_b, F)
                dve_sums_end(e, half_done, c, last_b, F)
                e.tensor_tensor(X[:, :], X[:, :], A[:, 0:NB * F], ALU.add)
                e.drain()
        layernorm("l3n", out)


def kernel(**inputs):
    import numpy as np
    from concourse import bacc
    from concourse.bass_utils import run_bass_kernel_spmd

    a = {n: np.ascontiguousarray(np.asarray(v)) for n, v in inputs.items()}

    def padded(v, n, fill):
        o = np.full((n,) + v.shape[1:], fill, v.dtype)
        o[:v.shape[0]] = v
        return o

    def columns(v):
        return np.ascontiguousarray(v.reshape(NG, P, TILES).transpose(1, 0, 2).reshape(P, NG * TILES))

    dst = padded(a["dst"], EP, PAD_NODE)
    attr = padded(a["edge_attr_64"], EP, 0).reshape(NG, P, TILES, N_RBF)
    attr_t = np.ascontiguousarray(attr.transpose(0, 2, 3, 1).reshape(NG, 2, TILES // 2, N_RBF, P)
                                  .transpose(0, 1, 3, 2, 4).reshape(NG, 2 * N_RBF, GE // 2))
    consts = np.zeros((P, C_WIDTH), np.float32)
    consts[:, C_IDENT:C_IDENT + P] = np.eye(P)
    consts[:, C_TRI:C_TRI + P] = np.triu(np.ones((P, P)), 1)
    consts[:, C_ONES:C_ONES + P] = 1.0
    consts[:, C_NODE:C_NODE + NB] = np.arange(P)[:, None] + P * np.arange(NB)[None, :]
    consts[:, C_GROUP:C_GROUP + 2] = GE * (np.arange(P)[:, None] + HG * np.arange(2)[None, :])
    for k in range(PARTS * TILES):
        if k % PARTS < 3:
            t = k // PARTS
            consts[k, C_SPREAD + t * P:C_SPREAD + (t + 1) * P] = 1.0
    feeds = {
        "x": padded(a["x"], NP_, 0),
        "src_c": columns(padded(a["src"], EP, PAD_NODE)),
        "dst_c": columns(dst),
        "type_c": columns(padded(a["edge_type_40"], EP, 0)),
        "weight_c": columns(padded(a["edge_weight"], EP, 0)),
        "dst_row": np.ascontiguousarray(dst.reshape(NG, P, TILES).transpose(0, 2, 1).reshape(NG, GE)),
        "attr_t": attr_t,
        "consts": consts,
        "iota": np.arange(NP_, dtype=np.float32)[None, :],
        "L0_gnn_W": a["L0_gnn_W"],
        "L0_gnn_Wt": np.ascontiguousarray(a["L0_gnn_W"].T),
        "attn": np.ascontiguousarray(a["L0_gnn_attn_w"].reshape(2, F).T),
        "rel_row": a["L0_gnn_rel_emb"].reshape(1, N_RELS),
        "b1_col": a["L3_gnn_b1"].reshape(P, 1),
        "L3_gnn_W1d": np.concatenate([a["L3_gnn_W1"]] * 2, axis=0),
        "L3_gnn_W2": a["L3_gnn_W2"],
        "L3_gnn_Wl": a["L3_gnn_Wl"],
    }
    for n in ("L1_gnn_W_l", "L1_gnn_W_r", "L2_gnn_W_rel1", "L2_gnn_W_root1", "L2_gnn_W_rel2", "L2_gnn_W_root2",
              "L2_gnn_W_rel3", "L2_gnn_W_root3"):
        feeds[n + "t"] = np.ascontiguousarray(a[n].T)
    for n in ("L0_gnn_bias_w", "L2_gnn_b_rel1", "L2_gnn_b_rel2", "L2_gnn_b_rel3", "L3_gnn_b2", "L3_gnn_bl"):
        feeds[n] = a[n].reshape(1, F)

    nc = bacc.Bacc("TRN2", target_bir_lowering=False, num_devices=1)
    T = {n: nc.dram_tensor("in_" + n, v.shape, mybir.dt.from_np(v.dtype), kind="ExternalInput").ap()
         for n, v in feeds.items()}
    out = nc.dram_tensor("out_0", (N_NODES, F), f32, kind="ExternalOutput").ap()
    build_program(nc, T, out)
    r = run_bass_kernel_spmd(nc, [{"in_" + n: v for n, v in feeds.items()}], core_ids=[0])
    return r.results[0]["out_0"]
```
